# Optimizing a Trainium2 kernel written in Bass

```python
import numpy as np
import jax
import jax.numpy as jnp

def _softmax(x, axis=-1):
    return jax.nn.softmax(x, axis=axis)

def _gelu(x):
    return jax.nn.gelu(x, approximate=True)

def _silu(x):
    return jax.nn.silu(x)

def _sigmoid(x):
    return jax.nn.sigmoid(x)

def _layernorm(x, axis=-1, eps=1e-05):
    m = jnp.mean(x, axis=axis, keepdims=True)
    v = jnp.var(x, axis=axis, keepdims=True)
    return (x - m) / jnp.sqrt(v + eps)

def _scatter_add(tgt, idx, src, axis=0):
    return tgt.at[idx].add(src)

def _segment_sum(src, seg, n):
    return jax.ops.segment_sum(src, seg, n)
kernel_name = 'mk_perceiver_d1_seqx_r2_e166c1'

def setup_inputs(seed: int=0):
    np.random.seed(seed)
    _w = jnp.asarray

    def _rec_inputs():
        import jax
        import jax.numpy as jnp
        _rk = jax.random.key(seed)
        x = -0.0002928 + 1 * jax.random.normal(jax.random.fold_in(_rk, 1), (4, 128, 512), jnp.float32)
        _lenS = 128 - jax.random.randint(jax.random.fold_in(_rk, 7), (4,), 0, max(1, 128 // 4) + 1, jnp.int32)
        _lenS2 = 2048 - jax.random.randint(jax.random.fold_in(_rk, 8), (4,), 0, max(1, 2048 // 4) + 1, jnp.int32)
        _ctx_1024P = jax.random.normal(jax.random.fold_in(_rk, 11), (4, 16, 512), jnp.float32)
        _ctx_1024c = jax.random.dirichlet(jax.random.fold_in(_rk, 511), 0.3 * jnp.ones((16,), jnp.float32), (4, 2048))
        _ctx_1024t = jnp.einsum('bsk,bkd->bsd', _ctx_1024c, _ctx_1024P)
        _ctx_1024t = _ctx_1024t * jax.lax.rsqrt(jnp.mean(jnp.square(_ctx_1024t)) + 1e-12) * 0.953939
        ctx_1024 = -1.39393e-06 + 0.999914 * (_ctx_1024t + 0.3 * jax.random.normal(jax.random.fold_in(_rk, 611), (4, 2048, 512), jnp.float32))
        return (x, ctx_1024)
    x, ctx_1024 = _rec_inputs()

    def _L0_xattn_setup():
        import jax, jax.numpy as jnp
        import numpy as np
        import math
        D_MODEL = 512
        N_HEADS = 16
        D_HEAD = D_MODEL // N_HEADS
        key = jax.random.key(seed)
        ks = jax.random.split(key, 11)
        N, L, S = (2, 1024, 1024)
        inp = {'queries': jax.random.normal(ks[0], (N, L, D_MODEL), dtype=jnp.float32), 'keys': jax.random.normal(ks[1], (N, S, D_MODEL), dtype=jnp.float32), 'values': jax.random.normal(ks[2], (N, S, D_MODEL), dtype=jnp.float32), 'Wq': jax.random.normal(ks[3], (D_MODEL, N_HEADS * D_HEAD), dtype=jnp.float32) / math.sqrt(D_MODEL), 'bq': jnp.zeros((N_HEADS * D_HEAD,), dtype=jnp.float32), 'Wk': jax.random.normal(ks[4], (D_MODEL, N_HEADS * D_HEAD), dtype=jnp.float32) / math.sqrt(D_MODEL), 'bk': jnp.zeros((N_HEADS * D_HEAD,), dtype=jnp.float32), 'Wv': jax.random.normal(ks[5], (D_MODEL, N_HEADS * D_HEAD), dtype=jnp.float32) / math.sqrt(D_MODEL), 'bv': jnp.zeros((N_HEADS * D_HEAD,), dtype=jnp.float32), 'Wo': jax.random.normal(ks[6], (N_HEADS * D_HEAD, D_MODEL), dtype=jnp.float32) / math.sqrt(N_HEADS * D_HEAD), 'bo': jnp.zeros((D_MODEL,), dtype=jnp.float32)}
        return inp
    _L0_xattn_all = _L0_xattn_setup()
    _L0_xattn_in = {k: v for k, v in _L0_xattn_all.items() if k in ('Wq', 'bq', 'Wk', 'bk', 'Wv', 'bv', 'Wo', 'bo')}
    del _L0_xattn_all

    def _L0_attn_setup():
        import jax, jax.numpy as jnp
        import numpy as np
        NUM_HEADS = 16
        HIDDEN = 512
        HEAD_DIM = HIDDEN // NUM_HEADS
        GROUP_SIZE = 128

        def _attention(q, k, v, head_dim):
            scores = jnp.einsum('bghqd,bghkd->bghqk', q, k) / head_dim ** 0.5
            w = jax.nn.softmax(scores, axis=-1)
            return jnp.einsum('bghqk,bghkd->bghqd', w, v)
        key = jax.random.key(seed)
        k1, k2, k3 = jax.random.split(key, 3)
        hidden_states = jax.random.normal(k1, (2, 4096, HIDDEN), dtype=jnp.float32)
        w_qkv = jax.random.normal(k2, (3 * HIDDEN, HIDDEN), dtype=jnp.float32) * 0.02
        b_qkv = jax.random.normal(k3, (3 * HIDDEN,), dtype=jnp.float32) * 0.02
        return {'hidden_states': hidden_states, 'w_qkv': w_qkv, 'b_qkv': b_qkv}
    _L0_attn_all = _L0_attn_setup()
    _L0_attn_in = {k: v for k, v in _L0_attn_all.items() if k in ('w_qkv', 'b_qkv')}
    del _L0_attn_all

    def _L0_ffn_setup():
        import jax, jax.numpy as jnp
        import numpy as np
        B, S, D, H, E = (4, 1024, 512, 1024, 8)
        key = jax.random.key(seed)
        ks = jax.random.split(key, 8)
        scale = 0.02
        return {'x': jax.random.normal(ks[0], (B, S, D), dtype=jnp.float32), 'Wr': jax.random.normal(ks[1], (D, E), dtype=jnp.float32) * scale, 'br': jnp.zeros((E,), dtype=jnp.float32), 'W1': jax.random.normal(ks[2], (E, D, H), dtype=jnp.float32) * scale, 'b1': jnp.zeros((E, H), dtype=jnp.float32), 'W2': jax.random.normal(ks[3], (E, H, D), dtype=jnp.float32) * scale, 'b2': jnp.zeros((E, D), dtype=jnp.float32)}
    _L0_ffn_all = _L0_ffn_setup()
    _L0_ffn_in = {k: v for k, v in _L0_ffn_all.items() if k in ('Wr', 'br', 'W1', 'b1', 'W2', 'b2')}
    del _L0_ffn_all
    return {'x': x, 'ctx_1024': ctx_1024, 'L0_xattn_Wq': _L0_xattn_in['Wq'], 'L0_xattn_bq': _L0_xattn_in['bq'], 'L0_xattn_Wk': _L0_xattn_in['Wk'], 'L0_xattn_bk': _L0_xattn_in['bk'], 'L0_xattn_Wv': _L0_xattn_in['Wv'], 'L0_xattn_bv': _L0_xattn_in['bv'], 'L0_xattn_Wo': _L0_xattn_in['Wo'], 'L0_xattn_bo': _L0_xattn_in['bo'], 'L0_attn_w_qkv': _L0_attn_in['w_qkv'], 'L0_attn_b_qkv': _L0_attn_in['b_qkv'], 'L0_ffn_Wr': _L0_ffn_in['Wr'], 'L0_ffn_br': _L0_ffn_in['br'], 'L0_ffn_W1': _L0_ffn_in['W1'], 'L0_ffn_b1': _L0_ffn_in['b1'], 'L0_ffn_W2': _L0_ffn_in['W2'], 'L0_ffn_b2': _L0_ffn_in['b2']}

def reference(x, ctx_1024, L0_xattn_Wq, L0_xattn_bq, L0_xattn_Wk, L0_xattn_bk, L0_xattn_Wv, L0_xattn_bv, L0_xattn_Wo, L0_xattn_bo, L0_attn_w_qkv, L0_attn_b_qkv, L0_ffn_Wr, L0_ffn_br, L0_ffn_W1, L0_ffn_b1, L0_ffn_W2, L0_ffn_b2):
    import jax
    import jax.numpy as jnp

    def _L0_xattn_ref(queries, keys, values, Wq, bq, Wk, bk, Wv, bv, Wo, bo):
        import jax, jax.numpy as jnp
        import numpy as np
        import math
        D_MODEL = 512
        N_HEADS = 16
        D_HEAD = D_MODEL // N_HEADS
        N, L, _ = queries.shape
        S = keys.shape[1]
        H, D = (N_HEADS, D_HEAD)
        q = (queries @ Wq + bq).reshape(N, L, H, D)
        k = (keys @ Wk + bk).reshape(N, S, H, D)
        v = (values @ Wv + bv).reshape(N, S, H, D)
        sm = jnp.einsum('nlhd,nshd->nlhs', q, k) / math.sqrt(D)
        sm = jax.nn.softmax(sm, axis=1)
        attn = jnp.einsum('nlhs,nshd->nlhd', sm, v).reshape(N, L, H * D)
        return attn @ Wo + bo

    def _L0_attn_ref(hidden_states, w_qkv, b_qkv):
        import jax, jax.numpy as jnp
        import numpy as np
        NUM_HEADS = 16
        HIDDEN = 512
        HEAD_DIM = HIDDEN // NUM_HEADS
        GROUP_SIZE = 128

        def _attention(q, k, v, head_dim):
            scores = jnp.einsum('bghqd,bghkd->bghqk', q, k) / head_dim ** 0.5
            w = jax.nn.softmax(scores, axis=-1)
            return jnp.einsum('bghqk,bghkd->bghqd', w, v)
        b, n, _ = hidden_states.shape
        h, d, G = (NUM_HEADS, HEAD_DIM, GROUP_SIZE)
        ng = n // G
        half = G // 2
        qkv = hidden_states @ w_qkv.T + b_qkv
        qkv = qkv.reshape(b, n, 3, h, d).transpose(2, 0, 3, 1, 4)
        q, k, v = (qkv[0], qkv[1], qkv[2])

        def grp(x):
            return x.reshape(b, h, ng, G, d).transpose(0, 2, 1, 3, 4)
        q, k, v = (grp(q), grp(k), grp(v))
        q1, q2 = (q[:, :, :, :half], q[:, :, :, half:])
        k1, k2 = (k[:, :, :, :half], k[:, :, :, half:])
        v1, v2 = (v[:, :, :, :half], v[:, :, :, half:])
        q2 = jnp.roll(q2, -half, axis=2)
        k2 = jnp.roll(k2, -half, axis=2)
        v2 = jnp.roll(v2, -half, axis=2)
        out1 = _attention(q1, k1, v1, d)
        out2 = _attention(q2, k2, v2, d)
        out = jnp.concatenate([out1, out2], axis=3)
        out = jnp.concatenate([out[:, :, :, :half], jnp.roll(out[:, :, :, half:], half, axis=2)], axis=3)
        out = out.transpose(0, 2, 1, 3, 4).reshape(b, n, h * d)
        return out

    def _L0_ffn_ref(x, Wr, br, W1, b1, W2, b2):
        import jax, jax.numpy as jnp
        import numpy as np
        B, S, D, H, E = (4, 1024, 512, 1024, 8)
        d = x.shape[-1]
        tokens = x.reshape(-1, d)
        logits = tokens @ Wr + br
        probs = jax.nn.softmax(logits, axis=-1)
        expert = jnp.argmax(probs, axis=-1)
        max_prob = jnp.take_along_axis(probs, expert[:, None], axis=-1)
        h = jax.nn.relu(jnp.einsum('td,edh->teh', tokens, W1) + b1[None])
        y = jnp.einsum('teh,ehd->ted', h, W2) + b2[None]
        out = jnp.take_along_axis(y, expert[:, None, None], axis=1)[:, 0, :]
        return (out * max_prob).reshape(x.shape)
    x = x + _L0_xattn_ref(_layernorm(x, axis=-1), ctx_1024, ctx_1024, L0_xattn_Wq, L0_xattn_bq, L0_xattn_Wk, L0_xattn_bk, L0_xattn_Wv, L0_xattn_bv, L0_xattn_Wo, L0_xattn_bo)
    x = x + _L0_attn_ref(_layernorm(x, axis=-1), L0_attn_w_qkv, L0_attn_b_qkv)
    x = x + _L0_ffn_ref(_layernorm(x, axis=-1), L0_ffn_Wr, L0_ffn_br, L0_ffn_W1, L0_ffn_b1, L0_ffn_W2, L0_ffn_b2)
    return x

_drawn_inputs = setup_inputs


def setup_inputs(seed=0):
    import zlib

    import numpy as np

    out = dict(_drawn_inputs(seed))
    spreads = {'L0_xattn_bq': (0.0, 0.8),
     'L0_xattn_bk': (0.0, 0.1),
     'L0_xattn_bv': (0.0, 0.1),
     'L0_xattn_bo': (0.0, 0.8),
     'L0_ffn_br': (0.0, 0.8),
     'L0_ffn_b1': (0.0, 0.8),
     'L0_ffn_b2': (0.0, 0.8)}
    factors = {'L0_attn_b_qkv': 8.0, 'L0_ffn_Wr': 8.0, 'L0_ffn_W1': 8.0, 'L0_ffn_W2': 8.0}
    for name, (base, spread) in spreads.items():
        noise = np.random.default_rng([zlib.crc32(name.encode()), seed]).standard_normal(out[name].shape)
        drawn = base * np.exp(spread * noise) if base else spread * noise
        out[name] = jnp.asarray(drawn.astype(out[name].dtype))
    for name, factor in factors.items():
        out[name] = (out[name] * factor).astype(out[name].dtype)
    return out
```

```python
import concourse.bass as bass
from concourse import mybir
from contextlib import ExitStack

F32 = mybir.dt.float32
F32R = mybir.dt.float32r
I32 = mybir.dt.int32
U32 = mybir.dt.uint32
ALU = mybir.AluOpType
ACT = mybir.ActivationFunctionType
AX = mybir.AxisListType.X

P = 128
NB, L, D = 4, 128, 512
S = 2048
H, DH = 16, 32
E, F = 8, 1024
C = D // P
G = 4
SB = 256
BLK = S // SB
TPB = SB // P
T = S // P
HALF = 64
J = F // P
SCALE = float(DH) ** -0.5
EPS = 1e-5
OVER = (NB * L - 1) // P
STEPS = E + OVER


def program(nc, x, ctx_t, wq, bq, wk, bk, wv, bv, wo, bo, wqkv_t, bqk, bv2, wr, br, w1, b1, w2, b2, out):
    es = ExitStack()
    with es:
        heads_d = nc.dram_tensor("local_heads", (NB, H, L, DH), F32, kind="Internal").ap()
        slots_x = nc.dram_tensor("slots_x", (STEPS * P, D), F32, kind="Internal").ap()
        slots_y = nc.dram_tensor("slots_y", (STEPS * P, D), F32, kind="Internal").ap()

        top = [-(-nc.sbuf_base // 32) * 32]
        at = {}

        def place(name, shape, dt, offset=None):
            size = 4
            for k in shape[1:]:
                size *= k
            if offset is None:
                offset = top[0]
                top[0] += -(-size // 32) * 32
            at[name] = offset
            return nc.alloc_sbuf_tensor_at(name, list(shape), dt, offset=offset)

        wk_hi = place("wk_hi", [P, C, D], F32R)
        wk_lo = place("wk_lo", [P, C, D], F32R)
        wv_hi = place("wv_hi", [P, C, D], F32R)
        wv_lo = place("wv_lo", [P, C, D], F32R)
        qd_hi = place("qd_hi", [P, G, G * L], F32R)
        qd_lo = place("qd_lo", [P, G, G * L], F32R)
        qf = place("qf", [P, G, NB * L], F32)
        v_raw = place("v_raw", [P, 4, D], F32)
        v_scaled = place("v_scaled", [P, 2, D], F32)
        e_sb = place("e_sb", [P, 2, H * L], F32)
        ctx_raw = place("ctx_raw", [P, 2, C * SB], F32)
        ctx_hi = place("ctx_hi", [P, 2, C * SB], F32R)
        ctx_lo = place("ctx_lo", [P, 2, C * SB], F32R)
        kt_hi = place("kt_hi", [P, 2, C, SB], F32R)
        kt_lo = place("kt_lo", [P, 2, C, SB], F32R)
        wqkv = place("wqkv", [P, C, 3 * D], F32)
        wo_sb = place("wo_sb", [P, C, D], F32)
        p_pad = place("p_pad", [P, H, L], F32)
        kd = place("kd", [P, G, G * L], F32)
        x_sb = place("x_sb", [P, NB, D], F32)
        xn = place("xn", [P, D], F32)
        xn_t = place("xn_t", [P, C, L], F32)
        q2t = place("q2t", [P, G, L], F32)
        v2 = place("v2", [P, D], F32)
        s2 = place("s2", [P, H, HALF], F32)
        p_t = place("p_t", [P, G, L], F32)
        o2 = place("o2", [P, D], F32)
        mixed = place("mixed", [P, D], F32)
        cur = place("cur", [P, D], F32)
        bv_row = place("bv_row", [P, D], F32)
        bv2_row = place("bv2_row", [P, D], F32)
        ident = place("ident", [P, P], F32)
        before = place("before", [P, P], F32)
        ones = place("ones", [P, P], F32)
        wr_sb = place("wr_sb", [P, C, E], F32)
        br_row = place("br_row", [P, E], F32)
        bq_col = place("bq_col", [P, C], F32)
        bk_col = place("bk_col", [P, C], F32)
        bqk_col = place("bqk_col", [P, 2 * C], F32)
        nmax = place("nmax", [P, 2, H], F32)
        zsum = place("zsum", [P, 2, H], F32)
        rz = place("rz", [P, 2, H], F32)
        stats = place("stats", [P, 6], F32)
        mv = place("mv", [P, 2], F32)
        var_eps = place("var_eps", [P, 1], F32)
        rstd = place("rstd", [P, 1], F32)
        power = place("power", [P, 1], F32)
        nm2 = place("nm2", [P, H], F32)
        z2 = place("z2", [P, H], F32)
        rz2 = place("rz2", [P, H], F32)
        mean_all = place("mean_all", [P, NB], F32)
        rstd_all = place("rstd_all", [P, NB], F32)
        logits = place("logits", [P, NB, E], F32)
        assert top[0] <= nc.sbuf_usable_end, (top[0], nc.sbuf_usable_end)
        wkv_raw = place("wkv_raw", [P, 2, C, D], F32, at["e_sb"])
        wq_sb = place("wq_sb", [P, C, D], F32, at["p_pad"])
        xt_all = place("xt_all", [P, C, NB * L], F32, at["kd"])
        attn_t = place("attn_t", [P, G, L], F32, at["s2"])
        bo_row = place("bo_row", [P, D], F32, at["o2"])
        w1_sb = [place("w1_0", [P, C, F], F32, at["wk_hi"]), place("w1_1", [P, C, F], F32, at["qd_hi"])]
        w2_sb = [place("w2_0", [P, J, D], F32, at["wv_hi"]), place("w2_1", [P, J, D], F32, at["qf"])]
        high = [at["e_sb"]]

        def over(name, shape, dt=F32):
            size = 4
            for k in shape[1:]:
                size *= k
            t = place(name, shape, dt, high[0])
            high[0] += -(-size // 32) * 32
            assert high[0] <= at["wqkv"]
            return t

        b1_sb = [over(f"b1_{i}", [P, J]) for i in range(2)]
        b2_sb = [over(f"b2_{i}", [P, D]) for i in range(2)]
        xs = [over(f"xs_{i}", [P, D]) for i in range(2)]
        y_sb = [over(f"y_{i}", [P, D]) for i in range(2)]
        xs_t = over("xs_t", [P, C, P])
        h_sb = over("h_sb", [P, F])
        h_t = over("h_t", [P, J, P])
        xf = over("xf", [P, NB, D])
        yg = over("yg", [P, NB, D])
        oh = over("oh", [P, NB, E])
        oh_idx = over("oh_idx", [P, NB, E])
        iota_e = over("iota_e", [P, E])
        r_a = over("r_a", [P, NB, E])
        r_b = over("r_b", [P, NB, E])
        pref = over("pref", [P, 2, NB * E])
        base = over("base", [P, NB, E])
        cnt = over("cnt", [P, E])
        ov = over("ov", [P, 3, E])
        cum = over("cum", [P, 2, E])
        tok = over("tok", [P, 6, NB])
        slot_i = over("slot_i", [P, NB], I32)
        maxl = over("maxl", [P, NB])
        rp = over("rp", [P, NB])
        plan = over("plan", [P, 4])
        plan_i = over("plan_i", [P, 4], I32)

        def bank(name, shape):
            return es.enter_context(nc.psum_tensor(name, shape, F32))

        ps_proj = [bank(f"ps_proj{i}", [P, 512]) for i in range(2)]
        ps_s = [bank(f"ps_s{i}", [P, G, L]) for i in range(G)]
        ps_pv = bank("ps_pv", [P, G, L])
        ps_m = bank("ps_m", [P, 512])
        ps_m4 = ps_m[:, :].rearrange("p (g l) -> p g l", g=G)

        def sem(name):
            return es.enter_context(nc.semaphore(name))

        x_in, wkv_in, wq_in, consts_in, wqkv_in, wo_in, bo_in = (sem(n) for n in (
            "x_in", "wkv_in", "wq_in", "consts_in", "wqkv_in", "wo_in", "bo_in"))
        ctx_in = [sem("ctx_in0"), sem("ctx_in1")]
        masks, consts_set = sem("masks"), sem("consts_set")
        zeroed, xs_zeroed = sem("zeroed"), sem("xs_zeroed")
        dve_own, pool_own = sem("dve_own"), sem("pool_own")
        var_ready, rstd_ready, xn_ready, xt_done, xt_ready = (sem(n) for n in (
            "var_ready", "rstd_ready", "xn_ready", "xt_done", "xt_ready"))
        q_done, qf_ready, wkv_split, qd_ready, wq_free = (sem(n) for n in (
            "q_done", "qf_ready", "wkv_split", "qd_ready", "wq_free"))
        ctx_high = sem("ctx_high")
        ctx_split, k_done, v_done, k_ready, v_ready = (sem(n) for n in (
            "ctx_split", "k_done", "v_done", "k_ready", "v_ready"))
        s_done, max_done, exp_done, rz_ready, vs_ready, pv_done = (sem(n) for n in (
            "s_done", "max_done", "exp_done", "rz_ready", "vs_ready", "pv_done"))
        attn_ready, wo_done, x1n_ready, tr_done, tr_ready = (sem(n) for n in (
            "attn_ready", "wo_done", "x1n_ready", "tr_done", "tr_ready"))
        qkv2_done, qkv2_ready, s2_done, s2_read, s2_ready, p2_exp, p2_ready = (sem(n) for n in (
            "qkv2_done", "qkv2_ready", "s2_done", "s2_read", "s2_ready", "p2_exp", "p2_ready"))
        pt_done, pt_ready, o2_done, o2_read, heads_out, heads_in = (sem(n) for n in (
            "pt_done", "pt_ready", "o2_done", "o2_read", "heads_out", "heads_in"))
        lg_done, lg_ready = sem("lg_done"), sem("lg_ready")
        oh_ready, pref_done, plan_ready, xf_ready, scattered = (sem(n) for n in (
            "oh_ready", "pref_done", "plan_ready", "xf_ready", "scattered"))
        w_in = [sem("w_in0"), sem("w_in1")]
        xs_in = [sem("xs_in0"), sem("xs_in1")]
        y_out = [sem("y_out0"), sem("y_out1")]
        xst_done, xst_ready, h_done, h_ready, ht_done, ht_ready, y_done, y_ready = (sem(n) for n in (
            "xst_done", "xst_ready", "h_done", "h_ready", "ht_done", "ht_ready", "y_done", "y_ready"))
        o_w_in, o_xs_in, o_y_out = sem("o_w_in"), sem("o_xs_in"), sem("o_y_out")
        gathered, out_ready, stored = sem("gathered"), sem("out_ready"), sem("stored")

        block = es.enter_context(nc.Block())

        DVE_CHAIN = 70

        @block.sync
        def _(sp):
            sp.dma_start(x_sb[:, :, :], x.rearrange("n t d -> t n d")).then_inc(x_in, 16)
            sp.dma_start(bo_row[:, :], bo.partition_broadcast(P)).then_inc(bo_in, 16)
            sp.dma_start(wq_sb[:, :, :], wq.rearrange("(c p) n -> p c n", p=P)).then_inc(wq_in, 16)
            sp.dma_start(wkv_raw[:, 0], wk.rearrange("(c p) n -> p c n", p=P)).then_inc(wkv_in, 16)
            sp.dma_start(wkv_raw[:, 1], wv.rearrange("(c p) n -> p c n", p=P)).then_inc(wkv_in, 16)
            sp.dma_start(bq_col[:, :], bq).then_inc(consts_in, 16)
            sp.dma_start(bk_col[:, :], bk).then_inc(consts_in, 16)
            sp.dma_start(bqk_col[:, :], bqk).then_inc(consts_in, 16)
            sp.dma_start(wr_sb[:, :, :], wr.rearrange("(c p) n -> p c n", p=P)).then_inc(consts_in, 16)
            sp.dma_start(bv_row[:, :], bv.partition_broadcast(P)).then_inc(consts_in, 16)
            sp.dma_start(bv2_row[:, :], bv2.partition_broadcast(P)).then_inc(consts_in, 16)
            sp.dma_start(br_row[:, :], br.partition_broadcast(P)).then_inc(consts_in, 16)

            def load_ctx(n, b):
                if b >= 2:
                    sp.wait_ge(ctx_split, n * BLK + b - 1)
                else:
                    sp.wait_ge(ctx_split, n * BLK)
                sp.dma_start(ctx_raw[:, b % 2, :], ctx_t[n, b]).then_inc(ctx_in[b % 2], 16)

            def local_heads(n):
                sp.wait_ge(o2_read, (n + 1) * G)
                sp.dma_start(heads_d[n].rearrange("h t d -> t h d"),
                             o2[:, :].rearrange("t (h d) -> t h d", d=DH)).then_inc(heads_out, 16)
                sp.wait_ge(heads_out, n * 16 + 16)
                sp.dma_start(mixed[:, :], heads_d[n].rearrange("h t d -> (h t d)").rearrange("(p c) -> p c", c=D)
                             ).then_inc(heads_in, 16)

            sp.wait_ge(zeroed, 1)
            zeros = s2[:, :, :].rearrange("p h k -> p (h k)")[:, 0:D]
            for i in range(STEPS):
                sp.dma_start(slots_x[i * P:(i + 1) * P, :], zeros).then_inc(xs_zeroed, 16)
            for i in range(E, STEPS):
                sp.dma_start(slots_y[i * P:(i + 1) * P, :], zeros).then_inc(xs_zeroed, 16)
            with sp.Fori(0, NB) as n:
                for b in range(BLK):
                    load_ctx(n, b)
                local_heads(n)

            def load_weights(s, e, arrived):
                sp.dma_start(w1_sb[s][:, :, :], w1[e].rearrange("(c p) h -> p c h", p=P)).then_inc(arrived, 16)
                sp.dma_start(w2_sb[s][:, :, :], w2[e].rearrange("(j p) d -> p j d", p=P)).then_inc(arrived, 16)
                sp.dma_start(b1_sb[s][:, :], b1[e]).then_inc(arrived, 16)
                sp.dma_start(b2_sb[s][:, :], b2[e].partition_broadcast(P)).then_inc(arrived, 16)

            sp.wait_ge(v_done, NB * T)
            sp.wait_ge(s_done, NB * T * G)
            sp.wait_ge(pv_done, NB * T)
            load_weights(0, 0, w_in[0])
            load_weights(1, 1, w_in[1])
            sp.wait_ge(scattered, NB * 16)

            def load_slots(s, i, arrived):
                sp.dma_start(xs[s][:, :], slots_x[i * P:(i + 1) * P, :] if isinstance(i, int)
                             else slots_x.rearrange("(i p) d -> i p d", p=P)[i]).then_inc(arrived, 16)

            load_slots(0, 0, xs_in[0])
            load_slots(1, 1, xs_in[1])
            with sp.Fori(1, E // 2) as i:
                for s in range(2):
                    sp.wait_ge(y_ready, 2 * i + s - 1)
                    load_weights(s, 2 * i + s, w_in[s])
                    load_slots(s, 2 * i + s, xs_in[s])
            sp.wait_ge(plan_ready, 1)
            n_over = sp.value_load(plan_i[0:1, OVER:OVER + 1], min_val=0, max_val=OVER)
            with sp.If(n_over > 0):
                with sp.Fori(0, n_over) as i:
                    sp.wait_ge(y_ready, i + E)
                    e = sp.value_load(plan_i[0:1, bass.ds(i, 1)], min_val=0, max_val=E - 1)
                    load_weights(0, e, o_w_in)
                    load_slots(0, i + E, o_xs_in)
            sp.wait_ge(out_ready, 1)
            sp.dma_start(out.rearrange("n t d -> t n d"), yg[:, :, :]).then_inc(stored, 16)
            sp.wait_ge(stored, 16)

        @block.gpsimd
        def _(pool):
            nc.gpsimd.memset(ident[:, :], 0.0).then_inc(pool_own, 1)
            nc.gpsimd.memset(ones[:, :], 1.0).then_inc(pool_own, 1)
            nc.gpsimd.memset(power[:, :], -0.5).then_inc(pool_own, 1)
            pool.wait_ge(pool_own, 3)
            nc.gpsimd.affine_select(out=ident[:, :], in_=ident[:, :], compare_op=ALU.not_equal, fill=1.0,
                                    base=0, pattern=[[-1, P]], channel_multiplier=1).then_inc(masks, 1)
            nc.gpsimd.affine_select(out=before[:, :], in_=ones[:, :], compare_op=ALU.is_gt, fill=0.0,
                                    base=0, pattern=[[1, P]], channel_multiplier=-1).then_inc(masks, 1)

            def inverse_root(k):
                pool.wait_ge(var_ready, k + 1)
                nc.gpsimd.tensor_tensor(out=rstd[:, :], in0=var_eps[:, :], in1=power[:, :], op=ALU.pow
                                        ).then_inc(rstd_ready, 1)

            for n in range(NB):
                inverse_root(n)

            def split_low(n, b):
                pool.wait_ge(ctx_high, n * BLK + b + 1)
                nc.gpsimd.tensor_tensor(out=ctx_lo[:, b % 2, :], in0=ctx_raw[:, b % 2, :],
                                        in1=ctx_hi[:, b % 2, :].bitcast(F32), op=ALU.subtract
                                        ).then_inc(ctx_split, 1)

            def scale_v(n, t):
                pool.wait_ge(v_ready, n * T + t + 1)
                pool.wait_ge(rz_ready, n * T + t + 1)
                pool.wait_ge(pv_done, n * T + t - 1 if t >= 2 else n * T)
                nc.gpsimd.tensor_tensor(
                    out=v_scaled[:, t % 2, :].rearrange("p (h d) -> p h d", d=DH),
                    in0=v_raw[:, t % 4, :].rearrange("p (h d) -> p h d", d=DH),
                    in1=rz[:, t % 2, :].unsqueeze(2).to_broadcast([P, H, DH]), op=ALU.mult).then_inc(vs_ready, 1)

            with pool.Fori(0, NB) as n:
                split_low(n, 0)
                split_low(n, 1)
                for t in range(T):
                    scale_v(n, t)
                    if t % 2 and t // 2 + 2 < BLK:
                        split_low(n, t // 2 + 2)
                inverse_root(2 * n + NB)
                inverse_root(2 * n + NB + 1)

            pool.wait_ge(xs_zeroed, 16 * (STEPS + OVER))
            pool.wait_ge(xf_ready, 1)
            for n in range(NB):
                nc.gpsimd.indirect_dma_start(
                    out=slots_x, out_offset=bass.IndirectOffsetOnAxis(ap=slot_i[:, n:n + 1].bitcast(U32), axis=0),
                    in_=xf[:, n, :], in_offset=None).then_inc(scattered, 16)
            ys = slots_y.rearrange("(i p) d -> i p d", p=P)
            with pool.Fori(0, E // 2) as i:
                for s in range(2):
                    pool.wait_ge(y_ready, 2 * i + s + 1)
                    pool.dma_start(ys[2 * i + s], y_sb[s][:, :]).then_inc(y_out[s], 16)
            for s in range(2):
                pool.wait_ge(y_out[s], 16 * (E // 2))
            n_over = pool.value_load(plan_i[0:1, OVER:OVER + 1], min_val=0, max_val=OVER)
            with pool.If(n_over > 0):
                with pool.Fori(0, n_over) as i:
                    pool.wait_ge(y_ready, i + E + 1)
                    pool.dma_start(ys[i + E], y_sb[0][:, :]).then_inc(o_y_out, 16)
                    pool.wait_ge(o_y_out, i * 16 + 16)
            for n in range(NB):
                nc.gpsimd.indirect_dma_start(
                    out=yg[:, n, :], out_offset=None, in_=slots_y,
                    in_offset=bass.IndirectOffsetOnAxis(ap=slot_i[:, n:n + 1].bitcast(U32), axis=0)
                ).then_inc(gathered, 16)

        @block.scalar
        def _(act):
            act.dma_start(wo_sb[:, :, :], wo.rearrange("(c p) n -> p c n", p=P)).then_inc(wo_in, 16)
            act.dma_start(wqkv[:, :, :], wqkv_t.rearrange("(c p) n -> p c n", p=P)).then_inc(wqkv_in, 16)

            def exps(n, t):
                act.wait_ge(pv_done, n * T + t - 1 if t >= 2 else n * T)
                for g in range(G):
                    act.wait_ge(max_done, n * T * G + t * G + g + 1)
                    for k in range(G):
                        h = G * g + k
                        last = nc.scalar.activation(e_sb[:, t % 2, h * L:(h + 1) * L], ps_s[g][:, k, :], ACT.Exp,
                                                    bias=nmax[:, t % 2, h:h + 1], scale=1.0,
                                                    accum_out=zsum[:, t % 2, h:h + 1])
                    last.then_inc(exp_done, 1)

            def split_high(n, b):
                act.wait_ge(ctx_in[b % 2], (n * (BLK // 2) + b // 2) * 16 + 16)
                act.wait_ge(v_done, n * T + TPB * (b - 1) if b >= 2 else n * T)
                nc.scalar.activation(ctx_hi[:, b % 2, :], ctx_raw[:, b % 2, :], ACT.Copy).then_inc(ctx_high, 1)

            act.wait_ge(wkv_split, 2)
            with act.Fori(0, NB) as n:
                split_high(n, 0)
                split_high(n, 1)
                for t in range(T):
                    exps(n, t)
                    if t % 2 and t // 2 + 2 < BLK:
                        split_high(n, t // 2 + 2)
                act.wait_ge(s2_ready, n + 1)
                nc.scalar.activation(s2[:, :, :], s2[:, :, :], ACT.Exp, scale=SCALE).then_inc(p2_exp, 1)

            act.wait_ge(lg_ready, 1)
            nc.scalar.activation(r_b[:, :, :], r_a[:, :, :], ACT.Exp).then_inc(lg_ready, 1)

            def take_h(k):
                for half in range(2):
                    act.wait_ge(h_done, 2 * k + half + 1)
                    if half == 0:
                        act.wait_ge(ht_done, 2 * k)
                    nc.scalar.activation(h_sb[:, half * 512:(half + 1) * 512],
                                         ps_s[half][:, :, :].rearrange("p g l -> p (g l)"), ACT.Copy
                                         ).then_inc(h_ready, 1)

            with act.Fori(0, E) as k:
                take_h(k)
            n_over = act.value_load(plan_i[0:1, OVER:OVER + 1], min_val=0, max_val=OVER)
            with act.If(n_over > 0):
                with act.Fori(0, n_over) as i:
                    take_h(i + E)

        @block.vector
        def _(dve):
            own = [0, 0]

            def link(ins):
                own[1] += 1
                ins.then_inc(dve_own, 1)
                dve.wait_ge(dve_own, own[0] + own[1])

            link(nc.vector.memset(s2[:, :, :], 0.0))
            nc.vector.memset(qd_hi[:, :, :].bitcast(F32), 0.0).then_inc(zeroed, 1)
            link(nc.vector.memset(qd_lo[:, :, :].bitcast(F32), 0.0))

            def norm(row, k, ready):
                link(nc.vector.tensor_reduce(mv[:, 0:1], row, AX, ALU.add))
                link(nc.vector.tensor_scalar(mv[:, 0:1], mv[:, 0:1], 1.0 / D, None, ALU.mult))
                link(nc.vector.tensor_scalar(xn[:, :], row, mv[:, 0:1], None, ALU.subtract))
                link(nc.vector.tensor_tensor_reduce(out=mixed[:, :], in0=xn[:, :], in1=xn[:, :], scale=1.0, scalar=0.0,
                                                    op0=ALU.mult, op1=ALU.add, accum_out=mv[:, 1:2]))
                nc.vector.tensor_scalar(var_eps[:, :], mv[:, 1:2], 1.0 / D, EPS, ALU.mult, ALU.add
                                        ).then_inc(var_ready, 1)
                dve.wait_ge(rstd_ready, k + 1)
                nc.vector.tensor_scalar(xn[:, :], xn[:, :], rstd[:, :], None, ALU.mult).then_inc(ready, 1)

            dve.wait_ge(x_in, 16)
            for n in range(NB):
                if n:
                    dve.wait_ge(xt_done, n)
                norm(x_sb[:, n, :], n, xn_ready)
                dve.wait_ge(xt_done, n + 1)
                nc.vector.tensor_copy(xt_all[:, :, n * L:(n + 1) * L], ps_m4).then_inc(xt_ready, 1)
            dve.wait_ge(bo_in, 16)
            dve.wait_ge(xn_ready, NB)
            link(nc.vector.tensor_tensor(x_sb[:, :, :], x_sb[:, :, :],
                                         bo_row[:, :].unsqueeze(1).to_broadcast([P, NB, D]), ALU.add))
            dve.wait_ge(wkv_in, 32)
            for i, (hi, lo) in enumerate(((wk_hi, wk_lo), (wv_hi, wv_lo))):
                link(nc.vector.tensor_copy(hi[:, :, :], wkv_raw[:, i]))
                nc.vector.tensor_tensor(lo[:, :, :], wkv_raw[:, i], hi[:, :, :].bitcast(F32), ALU.subtract
                                        ).then_inc(wkv_split, 1)
            dve.wait_ge(consts_in, 7 * 16)
            for g in range(G):
                dve.wait_ge(q_done, g + 1)
                nc.vector.tensor_scalar(qf[:, g, :], ps_s[g][:, :, :].rearrange("p g l -> p (g l)"), bq_col[:, g:g + 1],
                                        SCALE, ALU.add, ALU.mult).then_inc(qf_ready, 1)
            dve.wait_ge(qf_ready, G)
            link(nc.vector.memset(kd[:, :, :], 0.0))
            link(nc.vector.memset(p_pad[:, :, :], 0.0))

            def queries(n):
                dve.wait_ge(s_done, n * T * G)
                for k in range(G):
                    r = slice(DH * k, DH * (k + 1))
                    last = nc.vector.tensor_scalar(qd_hi[r, :, k * L:(k + 1) * L], qf[r, :, bass.ds(n * L, L)], 1.0,
                                                   None, ALU.mult)
                link(last)
                for k in range(G):
                    r = slice(DH * k, DH * (k + 1))
                    last = nc.vector.tensor_tensor(qd_lo[r, :, k * L:(k + 1) * L], qf[r, :, bass.ds(n * L, L)],
                                                   qd_hi[r, :, k * L:(k + 1) * L].bitcast(F32), ALU.subtract)
                last.then_inc(qd_ready, 1)

            def take_k(n, b):
                dve.wait_ge(s_done, n * T * G + TPB * G * (b - 1) if b >= 2 else n * T * G)
                for i in range(2):
                    dve.wait_ge(k_done, n * 2 * BLK + 2 * b + i + 1)
                    for m in range(2):
                        c = 2 * i + m
                        last = nc.vector.tensor_scalar(kt_hi[:, b % 2, c, :], ps_proj[i][:, m * SB:(m + 1) * SB],
                                                       bk_col[:, c:c + 1], None, ALU.add)
                    link(last)
                    for m in range(2):
                        c = 2 * i + m
                        last = nc.vector.scalar_tensor_tensor(
                            kt_lo[:, b % 2, c, :], ps_proj[i][:, m * SB:(m + 1) * SB], bk_col[:, c:c + 1],
                            kt_hi[:, b % 2, c, :].bitcast(F32), ALU.add, ALU.subtract)
                    last.then_inc(k_ready, 1)

            def take_v(n, t):
                dve.wait_ge(v_done, n * T + t + 1)
                dve.wait_ge(vs_ready, n * T + t - 3 if t >= 4 else n * T)
                nc.vector.tensor_tensor(v_raw[:, t % 4, :], ps_proj[t % 2][:, :], bv_row[:, :], ALU.add
                                        ).then_inc(v_ready, 1)

            def maxima(n, t):
                for g in range(G):
                    dve.wait_ge(s_done, n * T * G + t * G + g + 1)
                    nc.vector.tensor_reduce(nmax[:, t % 2, G * g:G * (g + 1)], ps_s[g][:, :, :], AX, ALU.max,
                                            negate=True).then_inc(max_done, 1)

            def sums(n, t):
                dve.wait_ge(exp_done, n * T * G + (t + 1) * G)
                nc.vector.reciprocal(rz[:, t % 2, :], zsum[:, t % 2, :]).then_inc(rz_ready, 1)

            def local(n):
                dve.wait_ge(xs_zeroed, 16 * (STEPS + OVER))
                dve.wait_ge(pv_done, (n + 1) * T)
                nc.vector.tensor_copy(attn_t[:, :, :], ps_pv[:, :, :]).then_inc(attn_ready, 1)
                dve.wait_ge(wo_done, n + 1)
                row = cur[:, :]
                link(nc.vector.tensor_tensor(row, x_sb[:, n, :], ps_m[:, :], ALU.add))
                norm(row, 2 * n + NB, x1n_ready)
                dve.wait_ge(tr_done, 2 * n + 1)
                nc.vector.tensor_copy(xn_t[:, :, :], ps_m4).then_inc(tr_ready, 1)
                dve.wait_ge(qkv2_done, 3 * n + 1)
                nc.vector.tensor_tensor(q2t[:, :, :], ps_m4, bqk_col[:, 0:C].unsqueeze(2).to_broadcast([P, C, L]),
                                        ALU.add).then_inc(qkv2_ready, 1)
                dve.wait_ge(qkv2_done, 3 * n + 2)
                for k in range(G):
                    r = slice(DH * k, DH * (k + 1))
                    last = nc.vector.tensor_tensor(kd[r, :, k * L:(k + 1) * L], ps_m4[r],
                                                   bqk_col[r, C:2 * C].unsqueeze(2).to_broadcast([DH, C, L]), ALU.add)
                last.then_inc(qkv2_ready, 1)
                dve.wait_ge(qkv2_done, 3 * n + 3)
                nc.vector.tensor_tensor(v2[:, :], ps_m[:, :], bv2_row[:, :], ALU.add).then_inc(qkv2_ready, 1)
                for g in range(G):
                    dve.wait_ge(s2_done, n * G + g + 1)
                    nc.vector.tensor_copy(s2[0:HALF, G * g:G * (g + 1), :], ps_m4[0:HALF, :, 0:HALF])
                    nc.vector.tensor_copy(s2[HALF:P, G * g:G * (g + 1), :], ps_m4[HALF:P, :, HALF:L]
                                          ).then_inc(s2_read, 1)
                dve.wait_ge(s2_read, (n + 1) * G)
                link(nc.vector.tensor_reduce(nm2[:, :], s2[:, :, :], AX, ALU.max, negate=True))
                nc.vector.tensor_tensor(s2[:, :, :], s2[:, :, :], nm2[:, :].unsqueeze(2).to_broadcast([P, H, HALF]),
                                        ALU.add).then_inc(s2_ready, 1)
                dve.wait_ge(p2_exp, n + 1)
                link(nc.vector.tensor_reduce(z2[:, :], s2[:, :, :], AX, ALU.add))
                link(nc.vector.reciprocal(rz2[:, :], z2[:, :]))
                for a in range(2):
                    r = slice(HALF * a, HALF * (a + 1))
                    last = nc.vector.tensor_tensor(p_pad[r, :, HALF * a:HALF * (a + 1)], s2[r, :, :],
                                                   rz2[r, :].unsqueeze(2).to_broadcast([HALF, H, HALF]), ALU.mult)
                last.then_inc(p2_ready, 1)
                dve.wait_ge(heads_out, n * 16)
                for g in range(G):
                    dve.wait_ge(pt_done, n * G + g + 1)
                    nc.vector.tensor_copy(p_t[:, :, :], ps_m4).then_inc(pt_ready, 1)
                    dve.wait_ge(o2_done, n * G + g + 1)
                    nc.vector.tensor_copy(o2[:, g * P:(g + 1) * P], ps_m[:, 0:P]).then_inc(o2_read, 1)
                dve.wait_ge(heads_in, n * 16 + 16)
                nc.vector.tensor_tensor(x_sb[:, n, :], row, mixed[:, :], ALU.add)
                link(nc.vector.tensor_tensor(row, row, mixed[:, :], ALU.add))
                norm(row, 2 * n + NB + 1, x1n_ready)
                nc.vector.tensor_scalar(mean_all[:, bass.ds(n, 1)], mv[:, 0:1], 1.0, None, ALU.mult)
                link(nc.vector.tensor_scalar(rstd_all[:, bass.ds(n, 1)], rstd[:, :], 1.0, None, ALU.mult))
                dve.wait_ge(tr_done, 2 * n + 2)
                nc.vector.tensor_copy(xn_t[:, :, :], ps_m4).then_inc(tr_ready, 1)
                dve.wait_ge(lg_done, n + 1)
                link(nc.vector.tensor_tensor(logits[:, n, :], ps_m[:, 0:E], br_row[:, :], ALU.add))

            start = own[1]
            with dve.Fori(0, NB) as n:
                own[0], own[1] = n * DVE_CHAIN + start, 0
                queries(n)
                take_k(n, 0)
                take_v(n, 0)
                take_v(n, 1)
                for t in range(T):
                    maxima(n, t)
                    if t:
                        sums(n, t - 1)
                    b = t // 2 + 1
                    if b < BLK and t % 2 == 0:
                        take_k(n, b)
                    if b < BLK and t % 2:
                        take_v(n, 2 * b)
                        take_v(n, 2 * b + 1)
                sums(n, T - 1)
                local(n)
                while own[1] < DVE_CHAIN:
                    link(nc.vector.memset(stats[:, 0:1], 0.0))
                assert own[1] == DVE_CHAIN, own
            own[0], own[1] = start + NB * DVE_CHAIN, 0

            link(nc.vector.tensor_reduce(maxl[:, :], logits[:, :, :], AX, ALU.max))
            wide = maxl[:, :].unsqueeze(2).to_broadcast([P, NB, E])
            nc.vector.tensor_tensor(r_a[:, :, :], logits[:, :, :], wide, ALU.subtract).then_inc(lg_ready, 1)
            link(nc.vector.tensor_tensor(oh[:, :, :], logits[:, :, :], wide, ALU.is_ge))
            for e in range(E):
                last = nc.vector.memset(iota_e[:, e:e + 1], float(e - E))
            link(last)
            iota_w = iota_e[:, :].unsqueeze(1).to_broadcast([P, NB, E])
            link(nc.vector.tensor_tensor(oh_idx[:, :, :], oh[:, :, :], iota_w, ALU.mult))
            link(nc.vector.tensor_reduce(maxl[:, :], oh_idx[:, :, :], AX, ALU.min))
            nc.vector.tensor_tensor(oh[:, :, :], iota_w, wide, ALU.is_equal).then_inc(oh_ready, 1)
            dve.wait_ge(lg_ready, 2)
            link(nc.vector.tensor_reduce(tok[:, 0, :], r_b[:, :, :], AX, ALU.add))
            link(nc.vector.reciprocal(rp[:, :], tok[:, 0, :]))
            dve.wait_ge(pref_done, 1)
            nc.vector.tensor_copy(pref[:, 0, :], ps_proj[0][:, 0:NB * E])
            link(nc.vector.tensor_copy(pref[:, 1, :], ps_proj[0][:, NB * E:2 * NB * E]))
            whole = pref[:, 1, :].rearrange("p (n e) -> p n e", e=E)
            link(nc.vector.memset(base[:, 0, :], 0.0))
            for n in range(1, NB):
                link(nc.vector.tensor_tensor(base[:, n, :], base[:, n - 1, :], whole[:, n - 1, :], ALU.add))
            link(nc.vector.tensor_tensor(cnt[:, :], base[:, NB - 1, :], whole[:, NB - 1, :], ALU.add))
            link(nc.vector.tensor_tensor(base[:, :, :], base[:, :, :],
                                         pref[:, 0, :].rearrange("p (n e) -> p n e", e=E), ALU.add))
            link(nc.vector.tensor_tensor(oh_idx[:, :, :], oh[:, :, :], base[:, :, :], ALU.mult))
            link(nc.vector.tensor_reduce(tok[:, 1, :], oh_idx[:, :, :], AX, ALU.add))
            for i in range(OVER):
                last = nc.vector.tensor_scalar(ov[:, i, :], cnt[:, :], float((i + 1) * P), None, ALU.is_gt)
            link(last)
            link(nc.vector.tensor_tensor(ov[:, 0, :], ov[:, 0, :], ov[:, 1, :], ALU.add))
            link(nc.vector.tensor_tensor(ov[:, 0, :], ov[:, 0, :], ov[:, 2, :], ALU.add))
            link(nc.vector.tensor_copy(cum[:, 0, 0:1], ov[:, 0, 0:1]))
            for e in range(1, E):
                link(nc.vector.tensor_tensor(cum[:, 0, e:e + 1], cum[:, 0, e - 1:e], ov[:, 0, e:e + 1], ALU.add))
            link(nc.vector.tensor_tensor(cum[:, 1, :], cum[:, 0, :], ov[:, 0, :], ALU.subtract))
            for i in range(OVER):
                link(nc.vector.tensor_scalar(ov[:, 1, :], cum[:, 0, :], float(i), None, ALU.is_le))
                link(nc.vector.tensor_reduce(plan[:, i:i + 1], ov[:, 1, :], AX, ALU.add))
            link(nc.vector.tensor_scalar(plan[:, 0:OVER], plan[:, 0:OVER], float(E - 1), None, ALU.min))
            link(nc.vector.tensor_copy(plan[:, OVER:OVER + 1], cum[:, 0, E - 1:E]))
            link(nc.vector.tensor_scalar(iota_e[:, :], iota_e[:, :], float(E), float(P), ALU.add, ALU.mult))
            link(nc.vector.tensor_tensor(oh_idx[:, :, :], oh[:, :, :], iota_w, ALU.mult))
            link(nc.vector.tensor_reduce(tok[:, 2, :], oh_idx[:, :, :], AX, ALU.add))
            link(nc.vector.tensor_tensor(oh_idx[:, :, :], oh[:, :, :],
                                         cum[:, 1, :].unsqueeze(1).to_broadcast([P, NB, E]), ALU.mult))
            link(nc.vector.tensor_reduce(tok[:, 3, :], oh_idx[:, :, :], AX, ALU.add))
            link(nc.vector.tensor_scalar(tok[:, 3, :], tok[:, 3, :], float(E - 1), float(P), ALU.add, ALU.mult))
            link(nc.vector.tensor_tensor(tok[:, 3, :], tok[:, 3, :], tok[:, 2, :], ALU.subtract))
            link(nc.vector.tensor_scalar(tok[:, 4, :], tok[:, 1, :], float(P), None, ALU.is_ge))
            link(nc.vector.tensor_tensor(tok[:, 3, :], tok[:, 3, :], tok[:, 4, :], ALU.mult))
            link(nc.vector.tensor_tensor(tok[:, 3, :], tok[:, 3, :], tok[:, 2, :], ALU.add))
            link(nc.vector.tensor_tensor(tok[:, 3, :], tok[:, 3, :], tok[:, 1, :], ALU.add))
            link(nc.vector.tensor_copy(slot_i[:, :], tok[:, 3, :]))
            nc.vector.tensor_copy(plan_i[:, :], plan[:, :]).then_inc(plan_ready, 1)
            for n in range(NB):
                last = nc.vector.tensor_scalar(xf[:, n, :], x_sb[:, n, :], mean_all[:, n:n + 1], rstd_all[:, n:n + 1],
                                               ALU.subtract, ALU.mult)
            last.then_inc(xf_ready, 1)

            def expert(s, k, w, w_count):
                dve.wait_ge(xst_done, k + 1)
                nc.vector.tensor_copy(xs_t[:, :, :], ps_m4).then_inc(xst_ready, 1)
                dve.wait_ge(w, w_count)
                for i in range(2):
                    dve.wait_ge(ht_done, 2 * k + i + 1)
                    for j in range(4 * i, 4 * i + 4):
                        last = nc.vector.tensor_scalar(h_t[:, j, :], ps_s[2 + i][:, j % 4, :], b1_sb[s][:, j:j + 1],
                                                       0.0, ALU.add, ALU.max)
                    last.then_inc(ht_ready, 1)
                dve.wait_ge(y_done, k + 1)

            with dve.Fori(0, E // 2) as i:
                for s in range(2):
                    expert(s, 2 * i + s, w_in[s], i * 64 + 64)
                    dve.wait_ge(y_out[s], i * 16)
                    nc.vector.tensor_tensor(y_sb[s][:, :], ps_pv[:, :, :].rearrange("p g l -> p (g l)"),
                                            b2_sb[s][:, :], ALU.add).then_inc(y_ready, 1)
            n_over = dve.value_load(plan_i[0:1, OVER:OVER + 1], min_val=0, max_val=OVER)
            with dve.If(n_over > 0):
                with dve.Fori(0, n_over) as i:
                    expert(0, i + E, o_w_in, i * 64 + 64)
                    dve.wait_ge(y_out[0], 16 * (E // 2))
                    dve.wait_ge(o_y_out, i * 16)
                    nc.vector.tensor_tensor(y_sb[0][:, :], ps_pv[:, :, :].rearrange("p g l -> p (g l)"),
                                            b2_sb[0][:, :], ALU.add).then_inc(y_ready, 1)
            dve.wait_ge(gathered, 16 * NB)
            for n in range(NB):
                last = nc.vector.scalar_tensor_tensor(yg[:, n, :], yg[:, n, :], rp[:, n:n + 1], x_sb[:, n, :],
                                                      ALU.mult, ALU.add)
            last.then_inc(out_ready, 1)

        @block.tensor
        def _(pe):
            mm = nc.tensor.matmul
            pe.wait_ge(masks, 2)
            for n in range(NB):
                pe.wait_ge(xn_ready, n + 1)
                if n:
                    pe.wait_ge(xt_ready, n)
                for c in range(C):
                    last = nc.tensor.transpose(ps_m4[:, c, :], xn[:, c * P:(c + 1) * P], ident[:, :])
                last.then_inc(xt_done, 1)
            pe.wait_ge(xt_ready, NB)
            pe.wait_ge(wq_in, 16)
            for g in range(G):
                for c in range(C):
                    last = mm(ps_s[g][:, :, :].rearrange("p g l -> p (g l)"), wq_sb[:, c, g * P:(g + 1) * P],
                              xt_all[:, c, :], start=c == 0, stop=c == C - 1)
                last.then_inc(q_done, 1)
            pe.wait_ge(qf_ready, G)
            pe.wait_ge(wkv_split, 2)

            def project_k(n, b):
                pe.wait_ge(ctx_split, n * BLK + b + 1)
                for i in range(2):
                    pe.wait_ge(v_ready, n * T + TPB * (b - 1) + i + 1 if b else n * T)
                    for m in range(2):
                        cols = slice((2 * i + m) * P, (2 * i + m + 1) * P)
                        k = 0
                        for c in range(C):
                            rows = slice(c * SB, (c + 1) * SB)
                            for w, z in ((wk_hi, ctx_hi), (wk_hi, ctx_lo), (wk_lo, ctx_hi)):
                                last = mm(ps_proj[i][:, m * SB:(m + 1) * SB], w[:, c, cols], z[:, b % 2, rows],
                                          start=k == 0, stop=k == 3 * C - 1, skip_group_check=True)
                                k += 1
                    last.then_inc(k_done, 1)

            def project_v(n, b):
                for i in range(TPB):
                    pe.wait_ge(k_ready, n * 2 * BLK + 2 * b + i + 1)
                    k = 0
                    for c in range(C):
                        rows = slice(c * SB + i * P, c * SB + (i + 1) * P)
                        for z, w in ((ctx_hi, wv_hi), (ctx_hi, wv_lo), (ctx_lo, wv_hi)):
                            last = mm(ps_proj[i][:, :], z[:, b % 2, rows], w[:, c, :], start=k == 0,
                                      stop=k == 3 * C - 1)
                            k += 1
                    last.then_inc(v_done, 1)

            def scores(n, t):
                b, rows = t // TPB, slice((t % TPB) * P, (t % TPB + 1) * P)
                pe.wait_ge(k_ready, n * 2 * BLK + 2 * (b + 1))
                for g in range(G):
                    pe.wait_ge(exp_done, n * T * G + (t - 1) * G + g + 1 if t else n * T * G)
                    for k, (z, q) in enumerate(((kt_hi, qd_hi), (kt_hi, qd_lo), (kt_lo, qd_hi))):
                        last = mm(ps_s[g][:, :, :].rearrange("p g l -> p (g l)"), z[:, b % 2, g, rows], q[:, g, :],
                                  start=k == 0, stop=k == 2)
                    last.then_inc(s_done, 1)

            def weigh(n, t):
                pe.wait_ge(exp_done, n * T * G + (t + 1) * G)
                pe.wait_ge(vs_ready, n * T + t + 1)
                if t == 0:
                    pe.wait_ge(attn_ready, n)
                for g in range(G):
                    for k in range(G):
                        h = G * g + k
                        last = mm(ps_pv[DH * k:DH * (k + 1), g, :], v_scaled[:, t % 2, h * DH:(h + 1) * DH],
                                  e_sb[:, t % 2, h * L:(h + 1) * L], start=t == 0 and g == 0, stop=t == T - 1,
                                  skip_group_check=True)
                last.then_inc(pv_done, 1)

            def local(n):
                pe.wait_ge(wo_in, 16)
                pe.wait_ge(attn_ready, n + 1)
                for g in range(G):
                    last = mm(ps_m[:, :], attn_t[:, g, :], wo_sb[:, g, :], start=g == 0, stop=g == G - 1)
                last.then_inc(wo_done, 1)
                pe.wait_ge(x1n_ready, 2 * n + 1)
                for c in range(C):
                    last = nc.tensor.transpose(ps_m4[:, c, :], xn[:, c * P:(c + 1) * P], ident[:, :])
                last.then_inc(tr_done, 1)
                pe.wait_ge(tr_ready, 2 * n + 1)
                pe.wait_ge(wqkv_in, 16)
                for part in range(2):
                    if part:
                        pe.wait_ge(qkv2_ready, 3 * n + 1)
                    for m in range(C):
                        for c in range(C):
                            col = part * D + m * P
                            last = mm(ps_m4[:, m, :], wqkv[:, c, col:col + P], xn_t[:, c, :], start=c == 0,
                                      stop=c == C - 1, skip_group_check=True)
                    last.then_inc(qkv2_done, 1)
                pe.wait_ge(qkv2_ready, 3 * n + 2)
                for c in range(C):
                    last = mm(ps_m[:, :], xn_t[:, c, :], wqkv[:, c, 2 * D:3 * D], start=c == 0, stop=c == C - 1)
                last.then_inc(qkv2_done, 1)
                pe.wait_ge(qkv2_ready, 3 * n + 3)
                for g in range(G):
                    if g:
                        pe.wait_ge(s2_read, n * G + g)
                    mm(ps_m[:, :], q2t[:, g, :], kd[:, g, :], start=True, stop=True).then_inc(s2_done, 1)
                pe.wait_ge(p2_ready, n + 1)
                for g in range(G):
                    if g:
                        pe.wait_ge(o2_read, n * G + g)
                    for k in range(G):
                        last = nc.tensor.transpose(ps_m4[:, k, :], p_pad[:, G * g + k, :], ident[:, :])
                    last.then_inc(pt_done, 1)
                    pe.wait_ge(pt_ready, n * G + g + 1)
                    for k in range(G):
                        h = G * g + k
                        last = mm(ps_m[:, k * DH:(k + 1) * DH], p_t[:, k, :], v2[:, h * DH:(h + 1) * DH], start=True,
                                  stop=True, skip_group_check=True)
                    last.then_inc(o2_done, 1)
                pe.wait_ge(x1n_ready, 2 * n + 2)
                for c in range(C):
                    last = nc.tensor.transpose(ps_m4[:, c, :], xn[:, c * P:(c + 1) * P], ident[:, :])
                last.then_inc(tr_done, 1)
                pe.wait_ge(tr_ready, 2 * n + 2)
                for c in range(C):
                    last = mm(ps_m[:, 0:E], xn_t[:, c, :], wr_sb[:, c, :], start=c == 0, stop=c == C - 1)
                last.then_inc(lg_done, 1)

            with pe.Fori(0, NB) as n:
                project_k(n, 0)
                project_v(n, 0)
                pe.wait_ge(qd_ready, n + 1)
                for t in range(T):
                    scores(n, t)
                    b = t // 2 + 1
                    if b < BLK:
                        project_v(n, b) if t % 2 else project_k(n, b)
                    if t:
                        weigh(n, t - 1)
                weigh(n, T - 1)
                local(n)

            pe.wait_ge(oh_ready, 1)
            flat = oh[:, :, :].rearrange("p n e -> p (n e)")
            mm(ps_proj[0][:, 0:NB * E], before[:, :], flat, start=True, stop=True, skip_group_check=True)
            mm(ps_proj[0][:, NB * E:2 * NB * E], ones[:, :], flat, start=True, stop=True, skip_group_check=True
               ).then_inc(pref_done, 1)

            def expert(s, k, w, w_count, xi, x_count):
                pe.wait_ge(xi, x_count)
                pe.wait_ge(y_ready, k)
                for c in range(C):
                    last = nc.tensor.transpose(ps_m4[:, c, :], xs[s][:, c * P:(c + 1) * P], ident[:, :])
                last.then_inc(xst_done, 1)
                pe.wait_ge(xst_ready, k + 1)
                pe.wait_ge(w, w_count)
                for half in range(2):
                    for c in range(C):
                        last = mm(ps_s[half][:, :, :].rearrange("p g l -> p (g l)"), xs_t[:, c, :],
                                  w1_sb[s][:, c, half * 512:(half + 1) * 512], start=c == 0, stop=c == C - 1)
                    last.then_inc(h_done, 1)
                for i in range(2):
                    pe.wait_ge(h_ready, 2 * k + i + 1)
                    for j in range(4 * i, 4 * i + 4):
                        last = nc.tensor.transpose(ps_s[2 + i][:, j % 4, :], h_sb[:, j * P:(j + 1) * P], ident[:, :])
                    last.then_inc(ht_done, 1)
                for j in range(J):
                    if j % 4 == 0:
                        pe.wait_ge(ht_ready, 2 * k + j // 4 + 1)
                    last = mm(ps_pv[:, :, :].rearrange("p g l -> p (g l)"), h_t[:, j, :], w2_sb[s][:, j, :],
                              start=j == 0, stop=j == J - 1)
                last.then_inc(y_done, 1)

            with pe.Fori(0, E // 2) as i:
                for s in range(2):
                    expert(s, 2 * i + s, w_in[s], i * 64 + 64, xs_in[s], i * 16 + 16)
            n_over = pe.value_load(plan_i[0:1, OVER:OVER + 1], min_val=0, max_val=OVER)
            with pe.If(n_over > 0):
                with pe.Fori(0, n_over) as i:
                    expert(0, i + E, o_w_in, i * 64 + 64, o_xs_in, i * 16 + 16)


def kernel(x, ctx_1024, L0_xattn_Wq, L0_xattn_bq, L0_xattn_Wk, L0_xattn_bk, L0_xattn_Wv, L0_xattn_bv, L0_xattn_Wo,
           L0_xattn_bo, L0_attn_w_qkv, L0_attn_b_qkv, L0_ffn_Wr, L0_ffn_br, L0_ffn_W1, L0_ffn_b1, L0_ffn_W2,
           L0_ffn_b2):
    import numpy as np
    import concourse.bacc as bacc
    from concourse.bass_utils import run_bass_kernel_spmd

    a = np.asarray
    cols = lambda v, k: a(v).reshape(k, P).T
    data = {
        "x": a(x),
        "ctx_t": a(ctx_1024).reshape(NB, BLK, SB, C, P).transpose(0, 1, 4, 3, 2).reshape(NB, BLK, P, C * SB),
        "wq": a(L0_xattn_Wq), "bq": cols(L0_xattn_bq, C), "wk": a(L0_xattn_Wk), "bk": cols(L0_xattn_bk, C),
        "wv": a(L0_xattn_Wv), "bv": a(L0_xattn_bv), "wo": a(L0_xattn_Wo), "bo": a(L0_xattn_bo),
        "wqkv_t": a(L0_attn_w_qkv).T, "bqk": cols(a(L0_attn_b_qkv)[:2 * D], 2 * C), "bv2": a(L0_attn_b_qkv)[2 * D:],
        "wr": a(L0_ffn_Wr), "br": a(L0_ffn_br), "w1": a(L0_ffn_W1),
        "b1": a(L0_ffn_b1).reshape(E, J, P).transpose(0, 2, 1), "w2": a(L0_ffn_W2), "b2": a(L0_ffn_b2),
    }
    nc = bacc.Bacc("TRN2", target_bir_lowering=False, num_devices=1)
    arrays, args = {}, []
    for name, v in data.items():
        v = np.ascontiguousarray(v)
        arrays["in_" + name] = v
        args.append(nc.dram_tensor("in_" + name, v.shape, mybir.dt.from_np(v.dtype), kind="ExternalInput").ap())
    args.append(nc.dram_tensor("out_0", (NB, L, D), F32, kind="ExternalOutput").ap())
    program(nc, *args)
    r = run_bass_kernel_spmd(nc, [arrays], core_ids=[0])
    return r.results[0]["out_0"]
```

```python
import concourse.bass as bass
from concourse import mybir
from contextlib import ExitStack

F32 = mybir.dt.float32
F32R = mybir.dt.float32r
I32 = mybir.dt.int32
U32 = mybir.dt.uint32
ALU = mybir.AluOpType
ACT = mybir.ActivationFunctionType
AX = mybir.AxisListType.X

P = 128
NB, L, D = 4, 128, 512
S = 2048
H, DH = 16, 32
E, F = 8, 1024
C = D // P
G = 4
SB = 256
BLK = S // SB
TPB = SB // P
T = S // P
HALF = 64
J = F // P
SCALE = float(DH) ** -0.5
EPS = 1e-5
OVER = (NB * L - 1) // P
STEPS = E + OVER


def program(nc, x, ctx_t, wq, bq, wk, bk, wv, bv, wo, bo, wqkv_t, bqk, bv2, wr, br, w1, b1, w2, b2, out):
    es = ExitStack()
    with es:
        heads_d = nc.dram_tensor("local_heads", (NB, H, L, DH), F32, kind="Internal").ap()
        slots_x = nc.dram_tensor("slots_x", (STEPS * P, D), F32, kind="Internal").ap()
        slots_y = nc.dram_tensor("slots_y", (STEPS * P, D), F32, kind="Internal").ap()

        top = [-(-nc.sbuf_base // 32) * 32]
        at = {}

        def place(name, shape, dt, offset=None):
            size = 4
            for k in shape[1:]:
                size *= k
            if offset is None:
                offset = top[0]
                top[0] += -(-size // 32) * 32
            at[name] = offset
            return nc.alloc_sbuf_tensor_at(name, list(shape), dt, offset=offset)

        wk_hi = place("wk_hi", [P, C, D], F32R)
        wk_lo = place("wk_lo", [P, C, D], F32R)
        wv_hi = place("wv_hi", [P, C, D], F32R)
        wv_lo = place("wv_lo", [P, C, D], F32R)
        qd_hi = place("qd_hi", [P, G, G * L], F32R)
        qd_both = place("qd_both", [P, G, G * L], F32R)
        qf = place("qf", [P, G, NB * L], F32)
        v_raw = place("v_raw", [P, 4, D], F32)
        v_scaled = place("v_scaled", [P, 2, D], F32)
        e_sb = place("e_sb", [P, 2, H * L], F32)
        k_pair = place("k_pair", [P, 2, G, 2, L], F32R)
        ctx_hi = place("ctx_hi", [P, 2, C * SB], F32R)
        ctx_lo = place("ctx_lo", [P, 2, C * SB], F32R)
        ctx_raw = place("ctx_raw", [P, 2, C * SB], F32, at["ctx_lo"])
        kt_hi = place("kt_hi", [P, 2, C, SB], F32R)
        kt_lo = place("kt_lo", [P, 2, C, SB], F32R)
        wqkv = place("wqkv", [P, C, 3 * D], F32)
        wo_sb = place("wo_sb", [P, C, D], F32)
        p_pad = place("p_pad", [P, H, L], F32)
        kd = place("kd", [P, G, G * L], F32)
        x_sb = place("x_sb", [P, NB, D], F32)
        xn = place("xn", [P, D], F32)
        xn_t = place("xn_t", [P, C, L], F32)
        q2t = place("q2t", [P, G, L], F32)
        v2 = place("v2", [P, D], F32)
        s2 = place("s2", [P, H, HALF], F32)
        p_t = place("p_t", [P, G, L], F32)
        o2 = place("o2", [P, D], F32)
        mixed = place("mixed", [P, D], F32)
        cur = place("cur", [P, D], F32)
        bv_row = place("bv_row", [P, D], F32)
        bv2_row = place("bv2_row", [P, D], F32)
        ident = place("ident", [P, P], F32)
        before = place("before", [P, P], F32)
        ones = place("ones", [P, P], F32)
        wr_sb = place("wr_sb", [P, C, E], F32)
        br_row = place("br_row", [P, E], F32)
        bq_col = place("bq_col", [P, C], F32)
        bk_col = place("bk_col", [P, C], F32)
        bqk_col = place("bqk_col", [P, 2 * C], F32)
        nmax = place("nmax", [P, 2, H], F32)
        zsum = place("zsum", [P, 2, H], F32)
        rz = place("rz", [P, 2, H], F32)
        stats = place("stats", [P, 6], F32)
        mv = place("mv", [P, 2], F32)
        var_eps = place("var_eps", [P, 1], F32)
        rstd = place("rstd", [P, 1], F32)
        power = place("power", [P, 1], F32)
        nm2 = place("nm2", [P, H], F32)
        z2 = place("z2", [P, H], F32)
        rz2 = place("rz2", [P, H], F32)
        mean_all = place("mean_all", [P, NB], F32)
        rstd_all = place("rstd_all", [P, NB], F32)
        logits = place("logits", [P, NB, E], F32)
        assert top[0] <= nc.sbuf_usable_end, (top[0], nc.sbuf_usable_end)
        wkv_raw = place("wkv_raw", [P, 2, C, D], F32, at["e_sb"])
        wq_sb = place("wq_sb", [P, C, D], F32, at["p_pad"])
        attn_t = place("attn_t", [P, G, L], F32, at["s2"])
        bo_row = place("bo_row", [P, D], F32, at["o2"])
        p_t_last = place("p_t_last", [P, G, G, L], F32, at["e_sb"])
        w1_sb = [place(f"w1_{i}", [P, C, F], F32, at["wk_hi"] + 2 * i * 4 * C * F) for i in range(3)]
        w2_sb = [place(f"w2_{i}", [P, J, D], F32, at["wk_hi"] + (2 * i + 1) * 4 * C * F) for i in range(3)]
        high = [at["w2_2"] + 4 * J * D]

        def over(name, shape, dt=F32):
            size = 4
            for k in shape[1:]:
                size *= k
            t = place(name, shape, dt, high[0])
            high[0] += -(-size // 32) * 32
            assert high[0] <= at["wo_sb"]
            return t

        b1_sb = [over(f"b1_{i}", [P, J]) for i in range(3)]
        b2_sb = [over(f"b2_{i}", [P, D]) for i in range(3)]
        xs = [over(f"xs_{i}", [P, D]) for i in range(3)]
        y_sb = [over(f"y_{i}", [P, D]) for i in range(2)]
        xs_t = over("xs_t", [P, C, P])
        h_sb = over("h_sb", [P, F])
        h_t = over("h_t", [P, J, P])
        xf = over("xf", [P, NB, D])
        yg = over("yg", [P, NB, D])
        oh = over("oh", [P, NB, E])
        oh_idx = over("oh_idx", [P, NB, E])
        iota_e = over("iota_e", [P, E])
        r_a = over("r_a", [P, NB, E])
        r_b = over("r_b", [P, NB, E])
        pref = over("pref", [P, 2, NB * E])
        base = over("base", [P, NB, E])
        cnt = over("cnt", [P, E])
        ov = over("ov", [P, 3, E])
        cum = over("cum", [P, 2, E])
        tok = over("tok", [P, 6, NB])
        slot_i = over("slot_i", [P, NB], I32)
        maxl = over("maxl", [P, NB])
        rp = over("rp", [P, NB])
        plan = over("plan", [P, 4])
        plan_i = over("plan_i", [P, 4], I32)

        def bank(name, shape):
            return es.enter_context(nc.psum_tensor(name, shape, F32))

        ps_proj = [bank(f"ps_proj{i}", [P, 512]) for i in range(2)]
        ps_s = [bank(f"ps_s{i}", [P, G, L]) for i in range(G)]
        ps_pv = bank("ps_pv", [P, G, L])
        ps_m = bank("ps_m", [P, 512])
        ps_m4 = ps_m[:, :].rearrange("p (g l) -> p g l", g=G)

        def sem(name):
            return es.enter_context(nc.semaphore(name))

        x0_in, x_in, wk_in, wv_in, wq_in, consts_in, late_in, wqkv_in, wo_in, bo_in = (sem(n) for n in (
            "x0_in", "x_in", "wk_in", "wv_in", "wq_in", "consts_in", "late_in", "wqkv_in", "wo_in", "bo_in"))
        ctx_in = [sem("ctx_in0"), sem("ctx_in1")]
        masks, consts_set = sem("masks"), sem("consts_set")
        zeroed, xs_zeroed = sem("zeroed"), sem("xs_zeroed")
        y_zeroed = sem("y_zeroed")
        dve_own, pool_own = sem("dve_own"), sem("pool_own")
        var_ready, rstd_ready, xn_ready, xt_done, xt_ready = (sem(n) for n in (
            "var_ready", "rstd_ready", "xn_ready", "xt_done", "xt_ready"))
        q_done, qf_ready, wkv_split, qd_ready, qd_zeroed = (sem(n) for n in (
            "q_done", "qf_ready", "wkv_split", "qd_ready", "qd_zeroed"))
        x_biased, kd_zeroed, p_zeroed, ot_done, ot_ready = (sem(n) for n in (
            "x_biased", "kd_zeroed", "p_zeroed", "ot_done", "ot_ready"))
        ctx_high = sem("ctx_high")
        pair_in = [sem("pair_in0"), sem("pair_in1")]
        ctx_split, k_done, v_done, k_ready, v_ready = (sem(n) for n in (
            "ctx_split", "k_done", "v_done", "k_ready", "v_ready"))
        s_done, max_done, exp_done, rz_ready, vs_ready, pv_done = (sem(n) for n in (
            "s_done", "max_done", "exp_done", "rz_ready", "vs_ready", "pv_done"))
        attn_ready, wo_done, x1n_ready, tr_done, tr_ready = (sem(n) for n in (
            "attn_ready", "wo_done", "x1n_ready", "tr_done", "tr_ready"))
        qkv2_done, qkv2_ready, s2_done, s2_read, s2_ready, p2_exp, p2_ready = (sem(n) for n in (
            "qkv2_done", "qkv2_ready", "s2_done", "s2_read", "s2_ready", "p2_exp", "p2_ready"))
        pt_done, pt_ready, o2_done, o2_read, heads_out, heads_in = (sem(n) for n in (
            "pt_done", "pt_ready", "o2_done", "o2_read", "heads_out", "heads_in"))
        lg_done, lg_taken, lg_ready = sem("lg_done"), sem("lg_taken"), sem("lg_ready")
        oh_ready, pref_done, plan_ready, xf_ready, scattered = (sem(n) for n in (
            "oh_ready", "pref_done", "plan_ready", "xf_ready", "scattered"))
        up_in = [sem("up_in0"), sem("up_in1")]
        down_in = [sem("down_in0"), sem("down_in1")]
        xs_in = [sem("xs_in0"), sem("xs_in1")]
        y_out = [sem("y_out0"), sem("y_out1")]
        xst_done, xst_ready, h_done, h_ready, ht_done, ht_ready, y_done, y_ready = (sem(n) for n in (
            "xst_done", "xst_ready", "h_done", "h_ready", "ht_done", "ht_ready", "y_done", "y_ready"))
        o_w_in, o_xs_in = sem("o_w_in"), sem("o_xs_in")
        gathered, out_ready, stored = sem("gathered"), sem("out_ready"), sem("stored")

        block = es.enter_context(nc.Block())

        DVE_CHAIN = 31

        def wait(eng, s, value):
            if not isinstance(value, int) or value > 0:
                eng.wait_ge(s, value)

        FIRST, AFTER = -TPB, T - TPB
        AT_WO, AT_X1, AT_Q, AT_K, AT_V, AT_S, AT_P, AT_O, AT_X2, AT_LG = 2, 4, 5, 6, 7, 8, 15, 23, 27, 27
        AT_SUM, AT_X2_IN = 14, 25
        AT_NORM = {2: 1, 8: 2, 14: 3}
        AT_BIAS = 20

        @block.sync
        def _(sp):
            sp.dma_start(x_sb[:, 0, :], x[0]).then_inc(x0_in, 16)
            sp.dma_start(wkv_raw[:, 0], wk.rearrange("(c p) n -> p c n", p=P)).then_inc(wk_in, 16)

            def load_ctx(n, b):
                wait(sp, v_done, n * T + TPB * (b - 1))
                sp.dma_start(ctx_raw[:, b % 2, :], ctx_t[n, b]).then_inc(ctx_in[b % 2], 16)

            def load_pairs(n, b):
                sp.wait_ge(k_ready, n * 2 * BLK + 2 * b + 2)
                for i in range(TPB):
                    if i:
                        wait(sp, s_done, n * T * G + (TPB * b + i - 1) * G)
                    for pair in range(2):
                        for copy in range(2):
                            sp.dma_start(k_pair[HALF * copy:HALF * (copy + 1), i, :, pair, :].bitcast(F32),
                                         kt_hi[HALF * pair:HALF * (pair + 1), b % 2, :, i * P:(i + 1) * P].bitcast(F32)
                                         ).then_inc(pair_in[i], 16)

            def local_heads(n):
                sp.wait_ge(o2_read, n + 1)
                sp.dma_start(heads_d[n].rearrange("h t d -> t h d"),
                             o2[:, :].rearrange("t (h d) -> t h d", d=DH)).then_inc(heads_out, 16)
                sp.wait_ge(heads_out, n * 16 + 16)
                sp.dma_start(mixed[:, :], heads_d[n].rearrange("h t d -> (h t d)").rearrange("(p c) -> p c", c=D)
                             ).then_inc(heads_in, 16)

            load_ctx(0, 0)
            sp.dma_start(bq_col[:, :], bq).then_inc(consts_in, 16)
            sp.dma_start(bk_col[:, :], bk).then_inc(consts_in, 16)
            sp.dma_start(wq_sb[:, :, :], wq.rearrange("(c p) n -> p c n", p=P)).then_inc(wq_in, 16)
            sp.dma_start(wkv_raw[:, 1], wv.rearrange("(c p) n -> p c n", p=P)).then_inc(wv_in, 16)
            load_ctx(0, 1)
            sp.dma_start(bv_row[:, :], bv.partition_broadcast(P)).then_inc(consts_in, 16)
            sp.dma_start(x_sb[:, 1:NB, :], x[1:NB].rearrange("n t d -> t n d")).then_inc(x_in, 16)
            load_pairs(0, 0)
            sp.dma_start(bo_row[:, :], bo.partition_broadcast(P)).then_inc(bo_in, 16)
            sp.dma_start(bqk_col[:, :], bqk).then_inc(late_in, 16)
            sp.dma_start(wr_sb[:, :, :], wr.rearrange("(c p) n -> p c n", p=P)).then_inc(late_in, 16)
            sp.dma_start(bv2_row[:, :], bv2.partition_broadcast(P)).then_inc(late_in, 16)
            sp.dma_start(br_row[:, :], br.partition_broadcast(P)).then_inc(late_in, 16)
            for b in range(2, BLK):
                load_ctx(0, b)
                if b == 3:
                    sp.dma_start(wo_sb[:, :, :], wo.rearrange("(c p) n -> p c n", p=P)).then_inc(wo_in, 16)
                    sp.dma_start(wqkv[:, :, :], wqkv_t.rearrange("(c p) n -> p c n", p=P)).then_inc(wqkv_in, 16)
                if b == 5:
                    sp.wait_ge(zeroed, 1)
                    zeros = s2[:, :, :].rearrange("p h k -> p (h k)")[:, 0:D]
                    for i in range(STEPS):
                        sp.dma_start(slots_x[i * P:(i + 1) * P, :], zeros).then_inc(xs_zeroed, 16)
                load_pairs(0, b - 1)
            load_pairs(0, BLK - 1)
            with sp.Fori(1, NB) as n:
                load_ctx(n, 0)
                load_ctx(n, 1)
                for b in range(BLK):
                    load_pairs(n, b)
                    if b + 2 < BLK:
                        load_ctx(n, b + 2)
                    if b == BLK - 2:
                        local_heads(n - 1)

            def load_up(s, e, arrived):
                sp.dma_start(w1_sb[s][:, :, :], w1[e].rearrange("(c p) h -> p c h", p=P)).then_inc(arrived, 16)
                sp.dma_start(b1_sb[s][:, :], b1[e]).then_inc(arrived, 16)

            def load_down(s, e, arrived):
                sp.dma_start(w2_sb[s][:, :, :], w2[e].rearrange("(j p) d -> p j d", p=P)).then_inc(arrived, 16)
                sp.dma_start(b2_sb[s][:, :], b2[e].partition_broadcast(P)).then_inc(arrived, 16)

            def load_slots(s, i, arrived):
                sp.dma_start(xs[s][:, :], slots_x[i * P:(i + 1) * P, :] if isinstance(i, int)
                             else slots_x.rearrange("(i p) d -> i p d", p=P)[i]).then_inc(arrived, 16)

            sp.wait_ge(v_done, NB * T)
            sp.wait_ge(s_done, NB * T * G)
            sp.wait_ge(pv_done, NB * T)
            for s in range(2):
                load_up(s, s, up_in[s])
                load_down(s, s, down_in[s])
            local_heads(NB - 1)
            sp.wait_ge(scattered, NB * 16)
            load_slots(0, 0, xs_in[0])
            load_slots(1, 1, xs_in[1])
            sp.wait_ge(plan_ready, 1)
            n_over = sp.value_load(plan_i[0:1, OVER:OVER + 1], min_val=0, max_val=OVER)
            with sp.If(n_over > 0):
                e = sp.value_load(plan_i[0:1, 0:1], min_val=0, max_val=E - 1)
                load_up(2, e, o_w_in)
                load_down(2, e, o_w_in)
                load_slots(2, E, o_xs_in)
            with sp.Fori(1, E // 2) as i:
                for s in range(2):
                    sp.wait_ge(h_done, 4 * i + 2 * s - 2)
                    sp.wait_ge(ht_ready, 4 * i + 2 * s - 2)
                    load_up(s, 2 * i + s, up_in[s])
                    load_slots(s, 2 * i + s, xs_in[s])
                    sp.wait_ge(y_ready, 2 * i + s - 1)
                    load_down(s, 2 * i + s, down_in[s])
            with sp.If(n_over > 1):
                with sp.Fori(1, n_over) as i:
                    sp.wait_ge(y_ready, i + E)
                    e = sp.value_load(plan_i[0:1, bass.ds(i, 1)], min_val=0, max_val=E - 1)
                    load_up(2, e, o_w_in)
                    load_down(2, e, o_w_in)
                    load_slots(2, i + E, o_xs_in)
            sp.wait_ge(out_ready, 1)
            sp.dma_start(out.rearrange("n t d -> t n d"), yg[:, :, :]).then_inc(stored, 16)
            sp.wait_ge(stored, 16)

        @block.gpsimd
        def _(pool):
            nc.gpsimd.memset(ident[:, :], 0.0).then_inc(pool_own, 1)
            nc.gpsimd.memset(ones[:, :], 1.0).then_inc(pool_own, 1)
            nc.gpsimd.memset(power[:, :], -0.5).then_inc(pool_own, 1)
            pool.wait_ge(pool_own, 3)
            nc.gpsimd.affine_select(out=ident[:, :], in_=ident[:, :], compare_op=ALU.not_equal, fill=1.0,
                                    base=0, pattern=[[-1, P]], channel_multiplier=1).then_inc(masks, 1)
            nc.gpsimd.affine_select(out=before[:, :], in_=ones[:, :], compare_op=ALU.is_gt, fill=0.0,
                                    base=0, pattern=[[1, P]], channel_multiplier=-1).then_inc(masks, 1)

            def inverse_root(k):
                pool.wait_ge(var_ready, k + 1)
                nc.gpsimd.tensor_tensor(out=rstd[:, :], in0=var_eps[:, :], in1=power[:, :], op=ALU.pow
                                        ).then_inc(rstd_ready, 1)

            nc.gpsimd.memset(qd_hi[:, :, :].bitcast(F32), 0.0).then_inc(qd_zeroed, 1)
            nc.gpsimd.memset(qd_both[:, :, :].bitcast(F32), 0.0).then_inc(qd_zeroed, 1)
            inverse_root(0)

            def split_low(n, b):
                wait(pool, ctx_high, n * BLK + b + 1)
                nc.gpsimd.tensor_tensor(out=ctx_lo[:, b % 2, :], in0=ctx_raw[:, b % 2, :],
                                        in1=ctx_hi[:, b % 2, :].bitcast(F32), op=ALU.subtract
                                        ).then_inc(ctx_split, 1)

            def scale_v(n, t):
                pool.wait_ge(v_ready, n * T + t + 1)
                pool.wait_ge(rz_ready, n * T + t + 1)
                wait(pool, pv_done, n * T + t - 1)
                nc.gpsimd.tensor_tensor(
                    out=v_scaled[:, t % 2, :].rearrange("p (h d) -> p h d", d=DH),
                    in0=v_raw[:, t % 4, :].rearrange("p (h d) -> p h d", d=DH),
                    in1=rz[:, t % 2, :].unsqueeze(2).to_broadcast([P, H, DH]), op=ALU.mult).then_inc(vs_ready, 1)

            def batch(n, first):
                if first < 0:
                    split_low(n, 0)
                for t in range(first, AFTER):
                    scale_v(n, t)
                    if t % 2 == 0 and t // 2 + 2 < BLK:
                        split_low(n, t // 2 + 2)
                    if first < 0 and t in (AT_WO // 2 - 1, AT_X2_IN // 2 - 1):
                        inverse_root(2 * n + NB - 2 + (t > 0))
                    if first == 0 and 2 * t + 2 in AT_NORM:
                        inverse_root(AT_NORM[2 * t + 2])
                    if first == 0 and t == AT_BIAS // 2 - 1:
                        pool.wait_ge(bo_in, 16)
                        pool.wait_ge(xn_ready, NB)
                        nc.gpsimd.tensor_tensor(out=x_sb[:, :, :], in0=x_sb[:, :, :],
                                                in1=bo_row[:, :].unsqueeze(1).to_broadcast([P, NB, D]), op=ALU.add
                                                ).then_inc(x_biased, 1)
                        pool.wait_ge(q_done, NB)
                        nc.gpsimd.memset(p_pad[:, :, :], 0.0).then_inc(p_zeroed, 1)

            split_low(0, 0)
            nc.gpsimd.memset(s2[:, :, :], 0.0).then_inc(zeroed, 1)
            nc.gpsimd.memset(kd[:, :, :], 0.0).then_inc(kd_zeroed, 1)
            split_low(0, 1)
            pool.wait_ge(zeroed, 1)
            ys = slots_y.rearrange("(i p) d -> i p d", p=P)
            zeros = s2[:, :, :].rearrange("p h k -> p (h k)")[:, 0:D]
            for arrived, i in ((y_out[0], E), (y_out[1], E + 1), (y_zeroed, E + 2)):
                pool.dma_start(ys[i], zeros).then_inc(arrived, 16)
            batch(0, 0)
            with pool.Fori(1, NB) as n:
                batch(n, FIRST)
            scale_v(NB - 1, T - 2)
            scale_v(NB - 1, T - 1)
            inverse_root(3 * NB - 2)
            inverse_root(3 * NB - 1)

            pool.wait_ge(xs_zeroed, 16 * STEPS)
            pool.wait_ge(y_zeroed, 16)
            pool.wait_ge(xf_ready, 1)
            for n in range(NB):
                nc.gpsimd.indirect_dma_start(
                    out=slots_x, out_offset=bass.IndirectOffsetOnAxis(ap=slot_i[:, n:n + 1].bitcast(U32), axis=0),
                    in_=xf[:, n, :], in_offset=None).then_inc(scattered, 16)
            with pool.Fori(0, E // 2) as i:
                for s in range(2):
                    pool.wait_ge(y_ready, 2 * i + s + 1)
                    pool.dma_start(ys[2 * i + s], y_sb[s][:, :]).then_inc(y_out[s], 16)
            for s in range(2):
                pool.wait_ge(y_out[s], 16 * (E // 2 + 1))
            n_over = pool.value_load(plan_i[0:1, OVER:OVER + 1], min_val=0, max_val=OVER)
            with pool.If(n_over > 0):
                with pool.Fori(0, n_over) as i:
                    pool.wait_ge(y_ready, i + E + 1)
                    pool.dma_start(ys[i + E], y_sb[0][:, :]).then_inc(y_out[0], 16)
                    pool.wait_ge(y_out[0], i * 16 + 16 + 16 * (E // 2 + 1))
            for n in range(NB):
                nc.gpsimd.indirect_dma_start(
                    out=yg[:, n, :], out_offset=None, in_=slots_y,
                    in_offset=bass.IndirectOffsetOnAxis(ap=slot_i[:, n:n + 1].bitcast(U32), axis=0)
                ).then_inc(gathered, 16)

        @block.scalar
        def _(act):
            def exps(n, t):
                wait(act, pv_done, n * T + t - 1)
                for g in range(G):
                    act.wait_ge(max_done, n * T * G + t * G + g + 1)
                    for k in range(G):
                        h = G * g + k
                        last = nc.scalar.activation(e_sb[:, t % 2, h * L:(h + 1) * L], ps_s[g][:, k, :], ACT.Exp,
                                                    bias=nmax[:, t % 2, h:h + 1], scale=1.0,
                                                    accum_out=zsum[:, t % 2, h:h + 1])
                    last.then_inc(exp_done, 1)

            def split_high(n, b):
                act.wait_ge(ctx_in[b % 2], (n * (BLK // 2) + b // 2) * 16 + 16)
                wait(act, v_done, n * T + TPB * (b - 1))
                nc.scalar.activation(ctx_hi[:, b % 2, :], ctx_raw[:, b % 2, :], ACT.Copy).then_inc(ctx_high, 1)

            def local_exp(n):
                act.wait_ge(s2_ready, n + 1)
                nc.scalar.activation(s2[:, :, :], s2[:, :, :], ACT.Exp, scale=SCALE).then_inc(p2_exp, 1)

            def batch(n, first):
                if first < 0:
                    split_high(n, 0)
                for t in range(first, AFTER):
                    exps(n, t)
                    if t % 2 == 0 and t // 2 + 2 < BLK:
                        split_high(n, t // 2 + 2)
                    if first < 0 and t == AT_SUM // 2 - 1:
                        local_exp(n - 1)

            split_high(0, 0)
            split_high(0, 1)
            batch(0, 0)
            with act.Fori(1, NB) as n:
                batch(n, FIRST)
            exps(NB - 1, T - 2)
            exps(NB - 1, T - 1)
            local_exp(NB - 1)

            act.wait_ge(lg_ready, 1)
            nc.scalar.activation(r_b[:, :, :], r_a[:, :, :], ACT.Exp).then_inc(lg_ready, 1)

            def take_h(k):
                for half in range(2):
                    act.wait_ge(h_done, 2 * k + half + 1)
                    if half == 0:
                        wait(act, ht_done, 2 * k)
                    nc.scalar.activation(h_sb[:, half * 512:(half + 1) * 512],
                                         ps_s[half][:, :, :].rearrange("p g l -> p (g l)"), ACT.Copy
                                         ).then_inc(h_ready, 1)

            take_h(0)
            with act.Fori(1, E) as k:
                take_h(k)
            n_over = act.value_load(plan_i[0:1, OVER:OVER + 1], min_val=0, max_val=OVER)
            with act.If(n_over > 0):
                with act.Fori(0, n_over) as i:
                    take_h(i + E)

        @block.vector
        def _(dve):
            own = [0, 0]

            def link(ins):
                own[1] += 1
                ins.then_inc(dve_own, 1)
                dve.wait_ge(dve_own, own[0] + own[1])

            def norm(row, k, ready):
                link(nc.vector.tensor_reduce(mv[:, 0:1], row, AX, ALU.add))
                link(nc.vector.tensor_scalar(mv[:, 0:1], mv[:, 0:1], 1.0 / D, None, ALU.mult))
                link(nc.vector.tensor_scalar(xn[:, :], row, mv[:, 0:1], None, ALU.subtract))
                link(nc.vector.tensor_tensor_reduce(out=mixed[:, :], in0=xn[:, :], in1=xn[:, :], scale=1.0, scalar=0.0,
                                                    op0=ALU.mult, op1=ALU.add, accum_out=mv[:, 1:2]))
                nc.vector.tensor_scalar(var_eps[:, :], mv[:, 1:2], 1.0 / D, EPS, ALU.mult, ALU.add
                                        ).then_inc(var_ready, 1)
                dve.wait_ge(rstd_ready, k + 1)
                nc.vector.tensor_scalar(xn[:, :], xn[:, :], rstd[:, :], None, ALU.mult).then_inc(ready, 1)

            def take_xt(n):
                dve.wait_ge(xt_done, n + 1)
                wait(dve, q_done, n)
                nc.vector.tensor_copy(xn_t[:, :, :], ps_m4).then_inc(xt_ready, 1)

            def take_q(n):
                dve.wait_ge(q_done, n + 1)
                for g in range(G):
                    last = nc.vector.tensor_scalar(qf[:, g, n * L:(n + 1) * L], ps_m4[:, g, :], bq_col[:, g:g + 1],
                                                   SCALE, ALU.add, ALU.mult)
                last.then_inc(qf_ready, 1)

            def prepare(place):
                if place in AT_NORM:
                    n = AT_NORM[place]
                    dve.wait_ge(x_in, 16)
                    norm(x_sb[:, n, :], n, xn_ready)
                if place - 2 in AT_NORM:
                    take_xt(AT_NORM[place - 2])
                if place - 3 in AT_NORM:
                    take_q(AT_NORM[place - 3])

            def split_weights(i, arrived, hi, lo):
                dve.wait_ge(arrived, 16)
                link(nc.vector.tensor_copy(hi[:, :, :], wkv_raw[:, i]))
                nc.vector.tensor_tensor(lo[:, :, :], wkv_raw[:, i], hi[:, :, :].bitcast(F32), ALU.subtract
                                        ).then_inc(wkv_split, 1)

            def queries(n):
                wait(dve, s_done, n * T * G)
                dve.wait_ge(qd_zeroed, 2)
                dve.wait_ge(qf_ready, n + 1) if isinstance(n, int) else dve.wait_ge(qf_ready, NB)
                for k in range(G):
                    r = slice(DH * k, DH * (k + 1))
                    for qd in (qd_hi, qd_both):
                        last = nc.vector.tensor_scalar(qd[r, :, k * L:(k + 1) * L], qf[r, :, bass.ds(n * L, L)], 1.0,
                                                       None, ALU.mult)
                link(last)
                for k in range(G):
                    r = slice(DH * k, DH * (k + 1))
                    away = (DH * k + HALF) % P
                    last = nc.vector.tensor_tensor(qd_both[away:away + DH, :, k * L:(k + 1) * L],
                                                   qf[r, :, bass.ds(n * L, L)],
                                                   qd_hi[r, :, k * L:(k + 1) * L].bitcast(F32), ALU.subtract)
                last.then_inc(qd_ready, 1)

            def take_k(n, b):
                wait(dve, s_done, n * T * G + TPB * G * (b - 1))
                for i in range(2):
                    dve.wait_ge(k_done, n * 2 * BLK + 2 * b + i + 1)
                    for m in range(2):
                        c = 2 * i + m
                        last = nc.vector.tensor_scalar(kt_hi[:, b % 2, c, :], ps_proj[i][:, m * SB:(m + 1) * SB],
                                                       bk_col[:, c:c + 1], None, ALU.add)
                    link(last)
                    for m in range(2):
                        c = 2 * i + m
                        last = nc.vector.scalar_tensor_tensor(
                            kt_lo[:, b % 2, c, :], ps_proj[i][:, m * SB:(m + 1) * SB], bk_col[:, c:c + 1],
                            kt_hi[:, b % 2, c, :].bitcast(F32), ALU.add, ALU.subtract)
                    last.then_inc(k_ready, 1)

            def take_v(n, t):
                dve.wait_ge(v_done, n * T + t + 1)
                wait(dve, vs_ready, n * T + t - 3)
                nc.vector.tensor_tensor(v_raw[:, t % 4, :], ps_proj[t % 2][:, :], bv_row[:, :], ALU.add
                                        ).then_inc(v_ready, 1)

            def maxima(n, t):
                for g in range(G):
                    dve.wait_ge(s_done, n * T * G + t * G + g + 1)
                    nc.vector.tensor_reduce(nmax[:, t % 2, G * g:G * (g + 1)], ps_s[g][:, :, :], AX, ALU.max,
                                            negate=True).then_inc(max_done, 1)

            def sums(n, t):
                dve.wait_ge(exp_done, n * T * G + (t + 1) * G)
                nc.vector.reciprocal(rz[:, t % 2, :], zsum[:, t % 2, :]).then_inc(rz_ready, 1)

            def take_attn(n):
                dve.wait_ge(xs_zeroed, 16 * STEPS)
                dve.wait_ge(y_zeroed, 16)
                dve.wait_ge(y_out[0], 16)
                dve.wait_ge(y_out[1], 16)
                dve.wait_ge(pv_done, n * T + T)
                nc.vector.tensor_copy(attn_t[:, :, :], ps_pv[:, :, :]).then_inc(attn_ready, 1)

            def local(n, place):
                row = cur[:, :]
                last_batch = isinstance(n, int)

                def in_bank(g):
                    return ps_s[g][:, :, :] if last_batch else ps_m4

                if place == AT_WO:
                    dve.wait_ge(wo_done, n + 1)
                    dve.wait_ge(x_biased, 1)
                    dve.wait_ge(late_in, 4 * 16)
                    link(nc.vector.tensor_tensor(row, x_sb[:, n, :], ps_m[:, :], ALU.add))
                    norm(row, 2 * n + NB, x1n_ready)
                if place == AT_X1:
                    dve.wait_ge(tr_done, 2 * n + 1)
                    nc.vector.tensor_copy(xn_t[:, :, :], ps_m4).then_inc(tr_ready, 1)
                if place == AT_Q:
                    dve.wait_ge(qkv2_done, 3 * n + 1)
                    nc.vector.tensor_tensor(q2t[:, :, :], ps_m4, bqk_col[:, 0:C].unsqueeze(2).to_broadcast([P, C, L]),
                                            ALU.add).then_inc(qkv2_ready, 1)
                if place == AT_K:
                    dve.wait_ge(qkv2_done, 3 * n + 2)
                    dve.wait_ge(kd_zeroed, 1)
                    for k in range(G):
                        r = slice(DH * k, DH * (k + 1))
                        last = nc.vector.tensor_tensor(kd[r, :, k * L:(k + 1) * L], ps_m4[r],
                                                       bqk_col[r, C:2 * C].unsqueeze(2).to_broadcast([DH, C, L]),
                                                       ALU.add)
                    last.then_inc(qkv2_ready, 1)
                if place == AT_V:
                    dve.wait_ge(qkv2_done, 3 * n + 3)
                    nc.vector.tensor_tensor(v2[:, :], ps_m[:, :], bv2_row[:, :], ALU.add).then_inc(qkv2_ready, 1)
                if AT_S <= place < AT_S + G:
                    g = place - AT_S
                    dve.wait_ge(s2_done, n * G + g + 1)
                    nc.vector.tensor_copy(s2[0:HALF, G * g:G * (g + 1), :], in_bank(g)[0:HALF, :, 0:HALF])
                    nc.vector.tensor_copy(s2[HALF:P, G * g:G * (g + 1), :], in_bank(g)[HALF:P, :, HALF:L]
                                          ).then_inc(s2_read, 1)
                if place == AT_S + G - 1:
                    dve.wait_ge(s2_read, n * G + G)
                    link(nc.vector.tensor_reduce(nm2[:, :], s2[:, :, :], AX, ALU.max, negate=True))
                    nc.vector.tensor_tensor(s2[:, :, :], s2[:, :, :], nm2[:, :].unsqueeze(2).to_broadcast([P, H, HALF]),
                                            ALU.add).then_inc(s2_ready, 1)
                if place == AT_SUM:
                    dve.wait_ge(p2_exp, n + 1)
                    dve.wait_ge(p_zeroed, 1)
                    link(nc.vector.tensor_reduce(z2[:, :], s2[:, :, :], AX, ALU.add))
                    link(nc.vector.reciprocal(rz2[:, :], z2[:, :]))
                    for a in range(2):
                        r = slice(HALF * a, HALF * (a + 1))
                        last = nc.vector.tensor_tensor(p_pad[r, :, HALF * a:HALF * (a + 1)], s2[r, :, :],
                                                       rz2[r, :].unsqueeze(2).to_broadcast([HALF, H, HALF]), ALU.mult)
                    last.then_inc(p2_ready, 1)
                def take_p(g):
                    dve.wait_ge(pt_done, n * G + g + 1)
                    nc.vector.tensor_copy(p_t_last[:, g] if last_batch else p_t[:, :, :], in_bank(g)
                                          ).then_inc(pt_ready, 1)

                def take_heads(g):
                    dve.wait_ge(o2_done, n * G + g + 1)
                    nc.vector.tensor_copy(attn_t[:, g, :], in_bank(g)[:, 0, :]).then_inc(ot_ready, 1)

                if not last_batch and AT_P <= place < AT_P + 2 * G:
                    g = (place - AT_P) // 2
                    take_heads(g) if (place - AT_P) % 2 else take_p(g)
                if last_batch and place == AT_P:
                    for g in range(G):
                        take_p(g)
                    for g in range(G):
                        take_heads(g)
                if place == AT_O:
                    dve.wait_ge(ot_done, n + 1)
                    wait(dve, heads_out, n * 16)
                    nc.vector.tensor_copy(o2[:, :], ps_m[:, :]).then_inc(o2_read, 1)
                if place == AT_X2_IN:
                    dve.wait_ge(heads_in, n * 16 + 16)
                    nc.vector.tensor_tensor(x_sb[:, n, :], row, mixed[:, :], ALU.add)
                    link(nc.vector.tensor_tensor(row, row, mixed[:, :], ALU.add))
                    norm(row, 2 * n + NB + 1, x1n_ready)
                    nc.vector.tensor_scalar(mean_all[:, bass.ds(n, 1)], mv[:, 0:1], 1.0, None, ALU.mult)
                    link(nc.vector.tensor_scalar(rstd_all[:, bass.ds(n, 1)], rstd[:, :], 1.0, None, ALU.mult))
                if place == AT_X2:
                    dve.wait_ge(tr_done, 2 * n + 2)
                    nc.vector.tensor_copy(xn_t[:, :, :], ps_m4).then_inc(tr_ready, 1)
                if place == AT_LG:
                    dve.wait_ge(lg_done, n + 1)
                    nc.vector.tensor_tensor(logits[:, n, :], ps_m[:, 0:E], br_row[:, :], ALU.add).then_inc(lg_taken, 1)

            def batch(n, first):
                for t in range(first, AFTER):
                    b = t // 2 + 1
                    maxima(n, t)
                    if t or first:
                        sums(n, t - 1)
                    if t == -1:
                        queries(n)
                    if first == 0:
                        prepare(2 * t)
                    if first < 0:
                        local(n - 1, 2 * t)
                    if t % 2 == 0:
                        take_k(n, b)
                    else:
                        take_v(n, 2 * b)
                        take_v(n, 2 * b + 1)
                    if first < 0 and t == 0:
                        take_attn(n - 1)
                    if first < 0:
                        local(n - 1, 2 * t + 1)
                    else:
                        prepare(2 * t + 1)

            def chain(value, used):
                own[0], own[1] = value, used

            dve.wait_ge(x0_in, 16)
            norm(x_sb[:, 0, :], 0, xn_ready)
            split_weights(0, wk_in, wk_hi, wk_lo)
            take_xt(0)
            split_weights(1, wv_in, wv_hi, wv_lo)
            dve.wait_ge(consts_in, 3 * 16)
            take_k(0, 0)
            take_q(0)
            queries(0)
            take_v(0, 0)
            take_v(0, 1)
            batch(0, 0)
            start = own[1]
            with dve.Fori(1, NB) as n:
                chain((n - 1) * DVE_CHAIN + start, 0)
                batch(n, FIRST)
                assert own[1] == DVE_CHAIN, own
            chain(start + (NB - 1) * DVE_CHAIN, 0)
            maxima(NB - 1, T - 2)
            sums(NB - 1, T - 3)
            maxima(NB - 1, T - 1)
            sums(NB - 1, T - 2)
            sums(NB - 1, T - 1)
            take_attn(NB - 1)
            for place in range(2 * AFTER):
                local(NB - 1, place)

            dve.wait_ge(lg_taken, NB)
            link(nc.vector.tensor_reduce(maxl[:, :], logits[:, :, :], AX, ALU.max))
            wide = maxl[:, :].unsqueeze(2).to_broadcast([P, NB, E])
            nc.vector.tensor_tensor(r_a[:, :, :], logits[:, :, :], wide, ALU.subtract).then_inc(lg_ready, 1)
            link(nc.vector.tensor_tensor(oh[:, :, :], logits[:, :, :], wide, ALU.is_ge))
            for e in range(E):
                last = nc.vector.memset(iota_e[:, e:e + 1], float(e - E))
            link(last)
            iota_w = iota_e[:, :].unsqueeze(1).to_broadcast([P, NB, E])
            link(nc.vector.tensor_tensor(oh_idx[:, :, :], oh[:, :, :], iota_w, ALU.mult))
            link(nc.vector.tensor_reduce(maxl[:, :], oh_idx[:, :, :], AX, ALU.min))
            nc.vector.tensor_tensor(oh[:, :, :], iota_w, wide, ALU.is_equal).then_inc(oh_ready, 1)
            dve.wait_ge(lg_ready, 2)
            link(nc.vector.tensor_reduce(tok[:, 0, :], r_b[:, :, :], AX, ALU.add))
            link(nc.vector.reciprocal(rp[:, :], tok[:, 0, :]))
            dve.wait_ge(pref_done, 1)
            nc.vector.tensor_copy(pref[:, 0, :], ps_proj[0][:, 0:NB * E])
            link(nc.vector.tensor_copy(pref[:, 1, :], ps_proj[0][:, NB * E:2 * NB * E]))
            whole = pref[:, 1, :].rearrange("p (n e) -> p n e", e=E)
            link(nc.vector.memset(base[:, 0, :], 0.0))
            for n in range(1, NB):
                link(nc.vector.tensor_tensor(base[:, n, :], base[:, n - 1, :], whole[:, n - 1, :], ALU.add))
            link(nc.vector.tensor_tensor(cnt[:, :], base[:, NB - 1, :], whole[:, NB - 1, :], ALU.add))
            link(nc.vector.tensor_tensor(base[:, :, :], base[:, :, :],
                                         pref[:, 0, :].rearrange("p (n e) -> p n e", e=E), ALU.add))
            link(nc.vector.tensor_tensor(oh_idx[:, :, :], oh[:, :, :], base[:, :, :], ALU.mult))
            link(nc.vector.tensor_reduce(tok[:, 1, :], oh_idx[:, :, :], AX, ALU.add))
            for i in range(OVER):
                last = nc.vector.tensor_scalar(ov[:, i, :], cnt[:, :], float((i + 1) * P), None, ALU.is_gt)
            link(last)
            link(nc.vector.tensor_tensor(ov[:, 0, :], ov[:, 0, :], ov[:, 1, :], ALU.add))
            link(nc.vector.tensor_tensor(ov[:, 0, :], ov[:, 0, :], ov[:, 2, :], ALU.add))
            link(nc.vector.tensor_copy(cum[:, 0, 0:1], ov[:, 0, 0:1]))
            for e in range(1, E):
                link(nc.vector.tensor_tensor(cum[:, 0, e:e + 1], cum[:, 0, e - 1:e], ov[:, 0, e:e + 1], ALU.add))
            link(nc.vector.tensor_tensor(cum[:, 1, :], cum[:, 0, :], ov[:, 0, :], ALU.subtract))
            for i in range(OVER):
                link(nc.vector.tensor_scalar(ov[:, 1, :], cum[:, 0, :], float(i), None, ALU.is_le))
                link(nc.vector.tensor_reduce(plan[:, i:i + 1], ov[:, 1, :], AX, ALU.add))
            link(nc.vector.tensor_scalar(plan[:, 0:OVER], plan[:, 0:OVER], float(E - 1), None, ALU.min))
            link(nc.vector.tensor_copy(plan[:, OVER:OVER + 1], cum[:, 0, E - 1:E]))
            link(nc.vector.tensor_scalar(iota_e[:, :], iota_e[:, :], float(E), float(P), ALU.add, ALU.mult))
            link(nc.vector.tensor_tensor(oh_idx[:, :, :], oh[:, :, :], iota_w, ALU.mult))
            link(nc.vector.tensor_reduce(tok[:, 2, :], oh_idx[:, :, :], AX, ALU.add))
            link(nc.vector.tensor_tensor(oh_idx[:, :, :], oh[:, :, :],
                                         cum[:, 1, :].unsqueeze(1).to_broadcast([P, NB, E]), ALU.mult))
            link(nc.vector.tensor_reduce(tok[:, 3, :], oh_idx[:, :, :], AX, ALU.add))
            link(nc.vector.tensor_scalar(tok[:, 3, :], tok[:, 3, :], float(E - 1), float(P), ALU.add, ALU.mult))
            link(nc.vector.tensor_tensor(tok[:, 3, :], tok[:, 3, :], tok[:, 2, :], ALU.subtract))
            link(nc.vector.tensor_scalar(tok[:, 4, :], tok[:, 1, :], float(P), None, ALU.is_ge))
            link(nc.vector.tensor_tensor(tok[:, 3, :], tok[:, 3, :], tok[:, 4, :], ALU.mult))
            link(nc.vector.tensor_tensor(tok[:, 3, :], tok[:, 3, :], tok[:, 2, :], ALU.add))
            link(nc.vector.tensor_tensor(tok[:, 3, :], tok[:, 3, :], tok[:, 1, :], ALU.add))
            link(nc.vector.tensor_copy(slot_i[:, :], tok[:, 3, :]))
            nc.vector.tensor_copy(plan_i[:, :], plan[:, :]).then_inc(plan_ready, 1)
            for n in range(NB):
                last = nc.vector.tensor_scalar(xf[:, n, :], x_sb[:, n, :], mean_all[:, n:n + 1], rstd_all[:, n:n + 1],
                                               ALU.subtract, ALU.mult)
            last.then_inc(xf_ready, 1)

            def take_x(k):
                dve.wait_ge(xst_done, k + 1)
                nc.vector.tensor_copy(xs_t[:, :, :], ps_m4).then_inc(xst_ready, 1)

            def take_hidden(s, k, w, w_count):
                dve.wait_ge(w, w_count)
                for i in range(2):
                    dve.wait_ge(ht_done, 2 * k + i + 1)
                    for j in range(4 * i, 4 * i + 4):
                        last = nc.vector.tensor_scalar(h_t[:, j, :], ps_s[2 + i][:, j % 4, :], b1_sb[s][:, j:j + 1],
                                                       0.0, ALU.add, ALU.max)
                    last.then_inc(ht_ready, 1)

            def take_y(s, k, w, w_count, stores):
                dve.wait_ge(y_done, k + 1)
                dve.wait_ge(w, w_count)
                wait(dve, y_out[s % 2], stores)
                nc.vector.tensor_tensor(y_sb[s % 2][:, :], ps_pv[:, :, :].rearrange("p g l -> p (g l)"),
                                        b2_sb[s][:, :], ALU.add).then_inc(y_ready, 1)

            def step(s, k, i):
                take_x(k)
                if not isinstance(k, int) or k:
                    take_y(1 - s, k - 1, down_in[1 - s], (i + s) * 32, (i + s) * 16)
                take_hidden(s, k, up_in[s], i * 32 + 32)

            step(0, 0, 0)
            step(1, 1, 0)
            with dve.Fori(1, E // 2) as i:
                step(0, 2 * i, i)
                step(1, 2 * i + 1, i)
            take_y(1, E - 1, down_in[1], E // 2 * 32, E // 2 * 16)
            n_over = dve.value_load(plan_i[0:1, OVER:OVER + 1], min_val=0, max_val=OVER)
            with dve.If(n_over > 0):
                with dve.Fori(0, n_over) as i:
                    take_x(i + E)
                    take_hidden(2, i + E, o_w_in, i * 64 + 64)
                    take_y(2, i + E, o_w_in, i * 64 + 64, i * 16 + 16 * (E // 2 + 1))
            dve.wait_ge(gathered, 16 * NB)
            for n in range(NB):
                last = nc.vector.scalar_tensor_tensor(yg[:, n, :], yg[:, n, :], rp[:, n:n + 1], x_sb[:, n, :],
                                                      ALU.mult, ALU.add)
            last.then_inc(out_ready, 1)

        @block.tensor
        def _(pe):
            mm = nc.tensor.matmul
            pe.wait_ge(masks, 2)

            def transpose_xn(n):
                pe.wait_ge(xn_ready, n + 1)
                wait(pe, qf_ready, n)
                for c in range(C):
                    last = nc.tensor.transpose(ps_m4[:, c, :], xn[:, c * P:(c + 1) * P], ident[:, :])
                last.then_inc(xt_done, 1)

            def make_q(n):
                pe.wait_ge(xt_ready, n + 1)
                pe.wait_ge(wq_in, 16)
                for g in range(G):
                    for c in range(C):
                        last = mm(ps_m4[:, g, :], wq_sb[:, c, g * P:(g + 1) * P], xn_t[:, c, :], start=c == 0,
                                  stop=c == C - 1, skip_group_check=True)
                last.then_inc(q_done, 1)

            def prepare(place):
                if place - 2 in AT_NORM:
                    transpose_xn(AT_NORM[place - 2])
                if place - 3 in AT_NORM:
                    make_q(AT_NORM[place - 3])

            def project_k(n, b):
                pe.wait_ge(ctx_split, n * BLK + b + 1)
                pe.wait_ge(wkv_split, 1)
                for i in range(2):
                    wait(pe, v_ready, n * T + TPB * (b - 1) + i + 1)
                    for m in range(2):
                        cols = slice((2 * i + m) * P, (2 * i + m + 1) * P)
                        k = 0
                        for c in range(C):
                            rows = slice(c * SB, (c + 1) * SB)
                            for w, z in ((wk_hi, ctx_hi), (wk_hi, ctx_lo), (wk_lo, ctx_hi)):
                                last = mm(ps_proj[i][:, m * SB:(m + 1) * SB], w[:, c, cols], z[:, b % 2, rows],
                                          start=k == 0, stop=k == 3 * C - 1, skip_group_check=True)
                                k += 1
                    last.then_inc(k_done, 1)

            def project_v(n, b):
                pe.wait_ge(wkv_split, 2)
                for i in range(TPB):
                    pe.wait_ge(k_ready, n * 2 * BLK + 2 * b + i + 1)
                    k = 0
                    for c in range(C):
                        rows = slice(c * SB + i * P, c * SB + (i + 1) * P)
                        for z, w in ((ctx_hi, wv_hi), (ctx_hi, wv_lo), (ctx_lo, wv_hi)):
                            last = mm(ps_proj[i][:, :], z[:, b % 2, rows], w[:, c, :], start=k == 0,
                                      stop=k == 3 * C - 1)
                            k += 1
                    last.then_inc(v_done, 1)

            def scores(n, t):
                b, rows = t // TPB, slice((t % TPB) * P, (t % TPB + 1) * P)
                pe.wait_ge(qd_ready, n + (t >= 0))
                pe.wait_ge(k_ready, n * 2 * BLK + 2 * (b + 1))
                pe.wait_ge(pair_in[t % 2], (n * (T // 2) + t // 2 + 1) * 64)
                for g in range(G):
                    wait(pe, exp_done, n * T * G + (t - 1) * G + g + 1)
                    mm(ps_s[g][:, :, :].rearrange("p g l -> p (g l)"), kt_lo[:, b % 2, g, rows], qd_hi[:, g, :],
                       start=True, stop=False, skip_group_check=True)
                    for pair in range(2):
                        cols = slice(pair * 2 * L, (pair + 1) * 2 * L)
                        last = mm(ps_s[g][:, :, :].rearrange("p g l -> p (g l)")[:, cols], k_pair[:, t % 2, g, pair, :],
                                  qd_both[:, g, cols], start=False, stop=True, skip_group_check=True)
                    last.then_inc(s_done, 1)

            def weigh(n, t):
                pe.wait_ge(exp_done, n * T * G + (t + 1) * G)
                pe.wait_ge(vs_ready, n * T + t + 1)
                if t == 0:
                    wait(pe, attn_ready, n)
                for g in range(G):
                    for k in range(G):
                        h = G * g + k
                        last = mm(ps_pv[DH * k:DH * (k + 1), g, :], v_scaled[:, t % 2, h * DH:(h + 1) * DH],
                                  e_sb[:, t % 2, h * L:(h + 1) * L], start=t == 0 and g == 0, stop=t % T == T - 1,
                                  skip_group_check=True)
                last.then_inc(pv_done, 1)

            def local(n, place):
                last_batch = isinstance(n, int)

                def in_bank(g):
                    return ps_s[g][:, :, :] if last_batch else ps_m4

                if place == AT_WO:
                    pe.wait_ge(wo_in, 16)
                    pe.wait_ge(attn_ready, n + 1)
                    wait(pe, lg_taken, n)
                    for g in range(G):
                        last = mm(ps_m[:, :], attn_t[:, g, :], wo_sb[:, g, :], start=g == 0, stop=g == G - 1)
                    last.then_inc(wo_done, 1)
                if place in (AT_X1, AT_X2):
                    k = 2 * n + 1 + (place == AT_X2)
                    pe.wait_ge(x1n_ready, k)
                    for c in range(C):
                        last = nc.tensor.transpose(ps_m4[:, c, :], xn[:, c * P:(c + 1) * P], ident[:, :])
                    last.then_inc(tr_done, 1)
                if place in (AT_Q, AT_K):
                    if place == AT_Q:
                        pe.wait_ge(tr_ready, 2 * n + 1)
                        pe.wait_ge(wqkv_in, 16)
                    else:
                        pe.wait_ge(qkv2_ready, 3 * n + 1)
                    for m in range(C):
                        for c in range(C):
                            col = (place - AT_Q) * D + m * P
                            last = mm(ps_m4[:, m, :], wqkv[:, c, col:col + P], xn_t[:, c, :], start=c == 0,
                                      stop=c == C - 1, skip_group_check=True)
                    last.then_inc(qkv2_done, 1)
                if place == AT_V:
                    pe.wait_ge(qkv2_ready, 3 * n + 2)
                    for c in range(C):
                        last = mm(ps_m[:, :], xn_t[:, c, :], wqkv[:, c, 2 * D:3 * D], start=c == 0, stop=c == C - 1)
                    last.then_inc(qkv2_done, 1)
                if AT_S <= place < AT_S + G:
                    g = place - AT_S
                    if g and not last_batch:
                        pe.wait_ge(s2_read, n * G + g)
                    if g == 0:
                        pe.wait_ge(qkv2_ready, 3 * n + 3)
                    mm(in_bank(g).rearrange("p g l -> p (g l)"), q2t[:, g, :], kd[:, g, :], start=True, stop=True).then_inc(s2_done, 1)
                def transpose_p(g):
                    if g and not last_batch:
                        pe.wait_ge(ot_ready, n * G + g)
                    else:
                        pe.wait_ge(p2_ready, n + 1)
                    for k in range(G):
                        last = nc.tensor.transpose(in_bank(g)[:, k, :], p_pad[:, G * g + k, :], ident[:, :])
                    last.then_inc(pt_done, 1)

                def weigh_local(g):
                    pe.wait_ge(pt_ready, n * G + g + 1)
                    for k in range(G):
                        h = G * g + k
                        last = mm(in_bank(g)[DH * k:DH * (k + 1), 0, :], v2[:, h * DH:(h + 1) * DH],
                                  p_t_last[:, g, k, :] if last_batch else p_t[:, k, :], start=True, stop=True,
                                  skip_group_check=True)
                    last.then_inc(o2_done, 1)

                if not last_batch and AT_P <= place < AT_P + 2 * G:
                    g = (place - AT_P) // 2
                    weigh_local(g) if (place - AT_P) % 2 else transpose_p(g)
                if last_batch and place == AT_P:
                    for g in range(G):
                        transpose_p(g)
                    for g in range(G):
                        weigh_local(g)
                if place == AT_O:
                    pe.wait_ge(ot_ready, n * G + G)
                    for g in range(G):
                        last = nc.tensor.transpose(ps_m4[:, g, :], attn_t[:, g, :], ident[:, :])
                    last.then_inc(ot_done, 1)
                if place == AT_LG:
                    pe.wait_ge(tr_ready, 2 * n + 2)
                    for c in range(C):
                        last = mm(ps_m[:, 0:E], xn_t[:, c, :], wr_sb[:, c, :], start=c == 0, stop=c == C - 1)
                    last.then_inc(lg_done, 1)

            def batch(n, first):
                for t in range(first, AFTER):
                    b = t // 2 + 1
                    scores(n, t)
                    if first < 0:
                        local(n - 1, 2 * t)
                    else:
                        prepare(2 * t)
                    project_v(n, b) if t % 2 else project_k(n, b)
                    if t or first:
                        weigh(n, t - 1)
                    if first < 0:
                        local(n - 1, 2 * t + 1)
                    else:
                        prepare(2 * t + 1)

            transpose_xn(0)
            project_k(0, 0)
            make_q(0)
            project_v(0, 0)
            batch(0, 0)
            with pe.Fori(1, NB) as n:
                batch(n, FIRST)
            scores(NB - 1, T - 2)
            weigh(NB - 1, T - 3)
            scores(NB - 1, T - 1)
            weigh(NB - 1, T - 2)
            weigh(NB - 1, T - 1)
            for place in range(2 * AFTER):
                local(NB - 1, place)

            pe.wait_ge(oh_ready, 1)
            flat = oh[:, :, :].rearrange("p n e -> p (n e)")
            mm(ps_proj[0][:, 0:NB * E], before[:, :], flat, start=True, stop=True, skip_group_check=True)
            mm(ps_proj[0][:, NB * E:2 * NB * E], ones[:, :], flat, start=True, stop=True, skip_group_check=True
               ).then_inc(pref_done, 1)

            def transpose_x(s, k, arrived, count):
                pe.wait_ge(arrived, count)
                wait(pe, xst_ready, k)
                for c in range(C):
                    last = nc.tensor.transpose(ps_m4[:, c, :], xs[s][:, c * P:(c + 1) * P], ident[:, :])
                last.then_inc(xst_done, 1)

            def up(s, k, arrived, count):
                pe.wait_ge(xst_ready, k + 1)
                pe.wait_ge(arrived, count)
                for half in range(2):
                    wait(pe, h_ready, 2 * k)
                    for c in range(C):
                        last = mm(ps_s[half][:, :, :].rearrange("p g l -> p (g l)"), xs_t[:, c, :],
                                  w1_sb[s][:, c, half * 512:(half + 1) * 512], start=c == 0, stop=c == C - 1)
                    last.then_inc(h_done, 1)
                for i in range(2):
                    wait(pe, ht_ready, 2 * k)
                    pe.wait_ge(h_ready, 2 * k + i + 1)
                    for j in range(4 * i, 4 * i + 4):
                        last = nc.tensor.transpose(ps_s[2 + i][:, j % 4, :], h_sb[:, j * P:(j + 1) * P], ident[:, :])
                    last.then_inc(ht_done, 1)

            def down(s, k, arrived, count):
                pe.wait_ge(arrived, count)
                wait(pe, y_ready, k)
                for j in range(J):
                    if j % 4 == 0:
                        pe.wait_ge(ht_ready, 2 * k + j // 4 + 1)
                    last = mm(ps_pv[:, :, :].rearrange("p g l -> p (g l)"), h_t[:, j, :], w2_sb[s][:, j, :],
                              start=j == 0, stop=j == J - 1)
                last.then_inc(y_done, 1)

            def step(s, k, i):
                transpose_x(s, k, xs_in[s], i * 16 + 16)
                if not isinstance(k, int) or k:
                    down(1 - s, k - 1, down_in[1 - s], (i + s) * 32)
                up(s, k, up_in[s], i * 32 + 32)

            step(0, 0, 0)
            step(1, 1, 0)
            with pe.Fori(1, E // 2) as i:
                step(0, 2 * i, i)
                step(1, 2 * i + 1, i)
            down(1, E - 1, down_in[1], E // 2 * 32)
            n_over = pe.value_load(plan_i[0:1, OVER:OVER + 1], min_val=0, max_val=OVER)
            with pe.If(n_over > 0):
                with pe.Fori(0, n_over) as i:
                    transpose_x(2, i + E, o_xs_in, i * 16 + 16)
                    up(2, i + E, o_w_in, i * 64 + 64)
                    down(2, i + E, o_w_in, i * 64 + 64)


def kernel(x, ctx_1024, L0_xattn_Wq, L0_xattn_bq, L0_xattn_Wk, L0_xattn_bk, L0_xattn_Wv, L0_xattn_bv, L0_xattn_Wo,
           L0_xattn_bo, L0_attn_w_qkv, L0_attn_b_qkv, L0_ffn_Wr, L0_ffn_br, L0_ffn_W1, L0_ffn_b1, L0_ffn_W2,
           L0_ffn_b2):
    import numpy as np
    import concourse.bacc as bacc
    from concourse.bass_utils import run_bass_kernel_spmd

    a = np.asarray
    cols = lambda v, k: a(v).reshape(k, P).T
    data = {
        "x": a(x),
        "ctx_t": a(ctx_1024).reshape(NB, BLK, SB, C, P).transpose(0, 1, 4, 3, 2).reshape(NB, BLK, P, C * SB),
        "wq": a(L0_xattn_Wq), "bq": cols(L0_xattn_bq, C), "wk": a(L0_xattn_Wk), "bk": cols(L0_xattn_bk, C),
        "wv": a(L0_xattn_Wv), "bv": a(L0_xattn_bv), "wo": a(L0_xattn_Wo), "bo": a(L0_xattn_bo),
        "wqkv_t": a(L0_attn_w_qkv).T, "bqk": cols(a(L0_attn_b_qkv)[:2 * D], 2 * C), "bv2": a(L0_attn_b_qkv)[2 * D:],
        "wr": a(L0_ffn_Wr), "br": a(L0_ffn_br), "w1": a(L0_ffn_W1),
        "b1": a(L0_ffn_b1).reshape(E, J, P).transpose(0, 2, 1), "w2": a(L0_ffn_W2), "b2": a(L0_ffn_b2),
    }
    nc = bacc.Bacc("TRN2", target_bir_lowering=False, num_devices=1)
    arrays, args = {}, []
    for name, v in data.items():
        v = np.ascontiguousarray(v)
        arrays["in_" + name] = v
        args.append(nc.dram_tensor("in_" + name, v.shape, mybir.dt.from_np(v.dtype), kind="ExternalInput").ap())
    args.append(nc.dram_tensor("out_0", (NB, L, D), F32, kind="ExternalOutput").ap())
    program(nc, *args)
    r = run_bass_kernel_spmd(nc, [arrays], core_ids=[0])
    return r.results[0]["out_0"]
```

```python
import concourse.bass as bass
from concourse import mybir
from contextlib import ExitStack

F32 = mybir.dt.float32
F32R = mybir.dt.float32r
I32 = mybir.dt.int32
U32 = mybir.dt.uint32
ALU = mybir.AluOpType
ACT = mybir.ActivationFunctionType
AX = mybir.AxisListType.X

P = 128
NB, L, D = 4, 128, 512
S = 2048
H, DH = 16, 32
E, F = 8, 1024
C = D // P
G = 4
SB = 256
BLK = S // SB
TPB = SB // P
T = S // P
HALF = 64
J = F // P
SCALE = float(DH) ** -0.5
EPS = 1e-5
OVER = (NB * L - 1) // P
STEPS = E + OVER


def program(nc, x, ctx_t, wq, bq, wk, bk, wv, bv, wo, bo, wqkv_t, bqk, bv2, wr, br, w1, b1, w2, b2, out):
    es = ExitStack()
    with es:
        heads_d = nc.dram_tensor("local_heads", (NB, H, L, DH), F32, kind="Internal").ap()
        slots_x = nc.dram_tensor("slots_x", (STEPS * P, D), F32, kind="Internal").ap()
        slots_y = nc.dram_tensor("slots_y", (STEPS * P, D), F32, kind="Internal").ap()

        top = [-(-nc.sbuf_base // 32) * 32]
        at = {}

        def place(name, shape, dt, offset=None):
            size = 4
            for k in shape[1:]:
                size *= k
            if offset is None:
                offset = top[0]
                top[0] += -(-size // 32) * 32
            at[name] = offset
            return nc.alloc_sbuf_tensor_at(name, list(shape), dt, offset=offset)

        wk_hi = place("wk_hi", [P, C, D], F32R)
        wk_lo = place("wk_lo", [P, C, D], F32R)
        wv_hi = place("wv_hi", [P, C, D], F32R)
        wv_lo = place("wv_lo", [P, C, D], F32R)
        qd_hi = place("qd_hi", [P, G, G * L], F32R)
        qd_both = place("qd_both", [P, G, G * L], F32R)
        qf = place("qf", [P, G, NB * L], F32)
        v_raw = place("v_raw", [P, 4, D], F32)
        v_scaled = place("v_scaled", [P, 2, D], F32)
        e_sb = place("e_sb", [P, 2, H * L], F32)
        k_pair = place("k_pair", [P, 2, G, 2, L], F32R)
        ctx_hi = place("ctx_hi", [P, 2, C * SB], F32R)
        ctx_lo = place("ctx_lo", [P, 2, C * SB], F32R)
        ctx_raw = place("ctx_raw", [P, 2, C * SB], F32, at["ctx_lo"])
        kt_hi = place("kt_hi", [P, 2, C, SB], F32R)
        kt_lo = place("kt_lo", [P, 2, C, SB], F32R)
        wqkv = place("wqkv", [P, C, 3 * D], F32)
        wo_sb = place("wo_sb", [P, C, D], F32)
        p_pad = place("p_pad", [P, H, L], F32)
        kd = place("kd", [P, G, G * L], F32)
        x_sb = place("x_sb", [P, NB, D], F32)
        xn = place("xn", [P, D], F32)
        xn_t = place("xn_t", [P, C, L], F32)
        q2t = place("q2t", [P, G, L], F32)
        v2 = place("v2", [P, D], F32)
        s2 = place("s2", [P, H, HALF], F32)
        p_t = place("p_t", [P, G, L], F32)
        o2 = place("o2", [P, D], F32)
        mixed = place("mixed", [P, D], F32)
        cur = place("cur", [P, D], F32)
        bv_row = place("bv_row", [P, D], F32)
        bv2_row = place("bv2_row", [P, D], F32)
        ident = place("ident", [P, P], F32)
        before = place("before", [P, P], F32)
        ones = place("ones", [P, P], F32)
        wr_sb = place("wr_sb", [P, C, E], F32)
        br_row = place("br_row", [P, E], F32)
        bq_col = place("bq_col", [P, C], F32)
        bk_col = place("bk_col", [P, C], F32)
        bqk_col = place("bqk_col", [P, 2 * C], F32)
        nmax = place("nmax", [P, 2, H], F32)
        zsum = place("zsum", [P, 2, H], F32)
        rz = place("rz", [P, 2, H], F32)
        mv = place("mv", [P, 2], F32)
        var_eps = place("var_eps", [P, 1], F32)
        rstd = place("rstd", [P, 1], F32)
        power = place("power", [P, 1], F32)
        nm2 = place("nm2", [P, H], F32)
        z2 = place("z2", [P, H], F32)
        rz2 = place("rz2", [P, H], F32)
        mean_all = place("mean_all", [P, NB], F32)
        rstd_all = place("rstd_all", [P, NB], F32)
        logits = place("logits", [P, NB, E], F32)
        assert top[0] <= nc.sbuf_usable_end, (top[0], nc.sbuf_usable_end)
        wkv_raw = place("wkv_raw", [P, 2, C, D], F32, at["e_sb"])
        wq_sb = place("wq_sb", [P, C, D], F32, at["p_pad"])
        attn_t = place("attn_t", [P, G, L], F32, at["s2"])
        bo_row = place("bo_row", [P, D], F32, at["o2"])
        p_t_last = place("p_t_last", [P, G, G, L], F32, at["e_sb"])
        w1_sb = [place(f"w1_{i}", [P, C, F], F32, at["wk_hi"] + 2 * i * 4 * C * F) for i in range(3)]
        w2_sb = [place(f"w2_{i}", [P, J, D], F32, at["wk_hi"] + (2 * i + 1) * 4 * C * F) for i in range(3)]
        high = [at["w2_2"] + 4 * J * D]

        def over(name, shape, dt=F32):
            size = 4
            for k in shape[1:]:
                size *= k
            t = place(name, shape, dt, high[0])
            high[0] += -(-size // 32) * 32
            assert high[0] <= at["wo_sb"]
            return t

        b1_sb = [over(f"b1_{i}", [P, J]) for i in range(3)]
        b2_sb = [over(f"b2_{i}", [P, D]) for i in range(3)]
        xs = [over(f"xs_{i}", [P, D]) for i in range(3)]
        y_sb = [over(f"y_{i}", [P, D]) for i in range(2)]
        xs_t = over("xs_t", [P, C, P])
        h_t = over("h_t", [P, J, P])
        xf = over("xf", [P, NB, D])
        yg = over("yg", [P, NB, D])
        oh = over("oh", [P, NB + 1, E])
        oh_idx = over("oh_idx", [P, NB, E])
        iota_e = over("iota_e", [P, E])
        r_a = over("r_a", [P, NB, E])
        r_b = over("r_b", [P, NB, E])
        over_cum = over("over_cum", [P, 2, E // 2 + E])
        over_off = over("over_off", [P, E])
        by_i = over("by_i", [P, OVER, E])
        rank = over("rank", [P, NB])
        chosen = over("chosen", [P, NB])
        first_slot = over("first_slot", [P, NB])
        beyond = over("beyond", [P, NB])
        moved = over("moved", [P, NB])
        esum = over("esum", [P, NB])
        slot_i = over("slot_i", [P, NB], I32)
        maxl = over("maxl", [P, NB])
        rp = over("rp", [P, NB])
        plan = over("plan", [P, 4])
        plan_i = over("plan_i", [P, 4], I32)

        def bank(name, shape):
            return es.enter_context(nc.psum_tensor(name, shape, F32))

        ps_proj = [bank(f"ps_proj{i}", [P, 512]) for i in range(2)]
        ps_s = [bank(f"ps_s{i}", [P, G, L]) for i in range(G)]
        ps_pv = bank("ps_pv", [P, G, L])
        ps_m = bank("ps_m", [P, 512])
        ps_m4 = ps_m[:, :].rearrange("p (g l) -> p g l", g=G)

        def sem(name):
            return es.enter_context(nc.semaphore(name))

        x0_in, x_in, wk_in, wv_in, wq_in, consts_in, late_in, wqkv_in, wo_in, bo_in = (sem(n) for n in (
            "x0_in", "x_in", "wk_in", "wv_in", "wq_in", "consts_in", "late_in", "wqkv_in", "wo_in", "bo_in"))
        ctx_in = [sem("ctx_in0"), sem("ctx_in1")]
        masks, consts_set = sem("masks"), sem("consts_set")
        zeroed, xs_zeroed = sem("zeroed"), sem("xs_zeroed")
        y_zeroed = sem("y_zeroed")
        dve_own, pool_own = sem("dve_own"), sem("pool_own")
        var_ready, rstd_ready, xn_ready, xt_done, xt_ready = (sem(n) for n in (
            "var_ready", "rstd_ready", "xn_ready", "xt_done", "xt_ready"))
        q_done, qf_ready, wkv_split, qd_ready, qd_zeroed = (sem(n) for n in (
            "q_done", "qf_ready", "wkv_split", "qd_ready", "qd_zeroed"))
        x_biased, kd_zeroed, p_zeroed, ot_done, ot_ready = (sem(n) for n in (
            "x_biased", "kd_zeroed", "p_zeroed", "ot_done", "ot_ready"))
        ctx_high = sem("ctx_high")
        pair_in = [sem("pair_in0"), sem("pair_in1")]
        ctx_split, k_done, v_done, k_ready, v_ready = (sem(n) for n in (
            "ctx_split", "k_done", "v_done", "k_ready", "v_ready"))
        s_done, max_done, exp_done, rz_ready, vs_ready, pv_done = (sem(n) for n in (
            "s_done", "max_done", "exp_done", "rz_ready", "vs_ready", "pv_done"))
        attn_ready, wo_done, x1n_ready, tr_done, tr_ready = (sem(n) for n in (
            "attn_ready", "wo_done", "x1n_ready", "tr_done", "tr_ready"))
        qkv2_done, qkv2_ready, s2_done, s2_read, s2_ready, p2_exp = (sem(n) for n in (
            "qkv2_done", "qkv2_ready", "s2_done", "s2_read", "s2_ready", "p2_exp"))
        pt_done, pt_ready, o2_done, o2_read, heads_out, heads_in = (sem(n) for n in (
            "pt_done", "pt_ready", "o2_done", "o2_read", "heads_out", "heads_in"))
        lg_done, lg_taken, lg_ready = sem("lg_done"), sem("lg_taken"), sem("lg_ready")
        oh_ready, pref_done, plan_ready, xf_ready, scattered = (sem(n) for n in (
            "oh_ready", "pref_done", "plan_ready", "xf_ready", "scattered"))
        up_in = [sem("up_in0"), sem("up_in1")]
        down_in = [sem("down_in0"), sem("down_in1")]
        xs_in = [sem("xs_in0"), sem("xs_in1")]
        y_out = [sem("y_out0"), sem("y_out1")]
        xst_done, xst_ready, ht_done, ht_ready, y_done, y_ready = (sem(n) for n in (
            "xst_done", "xst_ready", "ht_done", "ht_ready", "y_done", "y_ready"))
        o_w_in, o_xs_in = sem("o_w_in"), sem("o_xs_in")
        gathered = [sem(f"gathered{n}") for n in range(NB)]
        out_ready, stored = sem("out_ready"), sem("stored")

        block = es.enter_context(nc.Block())

        DVE_CHAIN = 32

        def wait(eng, s, value):
            if not isinstance(value, int) or value > 0:
                eng.wait_ge(s, value)

        FIRST, AFTER = -TPB - 1, T - TPB - 1
        AT_WO, AT_X1, AT_Q, AT_K, AT_V, AT_S, AT_P, AT_O, AT_X2, AT_LG = 2, 3, 4, 5, 6, 7, 14, 22, 25, 25
        AT_SUM, AT_X2_IN = 13, 24
        AT_NORM = {2: 1, 8: 2, 14: 3}
        AT_BIAS = 20

        @block.sync
        def _(sp):
            sp.dma_start(x_sb[:, 0, :], x[0]).then_inc(x0_in, 16)
            sp.dma_start(wkv_raw[:, 0], wk.rearrange("(c p) n -> p c n", p=P)).then_inc(wk_in, 16)

            def load_ctx(n, b):
                wait(sp, v_done, n * T + TPB * (b - 1))
                sp.dma_start(ctx_raw[:, b % 2, :], ctx_t[n, b]).then_inc(ctx_in[b % 2], 16)

            def load_pairs(n, b, tiles=range(TPB)):
                for i in tiles:
                    if i:
                        wait(sp, s_done, n * T * G + (TPB * b + i - 1) * G)
                    else:
                        sp.wait_ge(k_ready, n * 2 * BLK + 2 * b + 2)
                    for pair in range(2):
                        for copy in range(2):
                            sp.dma_start(k_pair[HALF * copy:HALF * (copy + 1), i, :, pair, :].bitcast(F32),
                                         kt_hi[HALF * pair:HALF * (pair + 1), b % 2, :, i * P:(i + 1) * P].bitcast(F32)
                                         ).then_inc(pair_in[i], 16)

            def local_heads(n):
                sp.wait_ge(o2_read, n + 1)
                sp.dma_start(heads_d[n].rearrange("h t d -> t h d"),
                             o2[:, :].rearrange("t (h d) -> t h d", d=DH)).then_inc(heads_out, 16)
                sp.wait_ge(heads_out, n * 16 + 16)
                sp.dma_start(mixed[:, :], heads_d[n].rearrange("h t d -> (h t d)").rearrange("(p c) -> p c", c=D)
                             ).then_inc(heads_in, 16)

            load_ctx(0, 0)
            sp.dma_start(bq_col[:, :], bq).then_inc(consts_in, 16)
            sp.dma_start(bk_col[:, :], bk).then_inc(consts_in, 16)
            sp.dma_start(wq_sb[:, :, :], wq.rearrange("(c p) n -> p c n", p=P)).then_inc(wq_in, 16)
            sp.dma_start(wkv_raw[:, 1], wv.rearrange("(c p) n -> p c n", p=P)).then_inc(wv_in, 16)
            load_ctx(0, 1)
            sp.dma_start(bv_row[:, :], bv.partition_broadcast(P)).then_inc(consts_in, 16)
            sp.dma_start(x_sb[:, 1:NB, :], x[1:NB].rearrange("n t d -> t n d")).then_inc(x_in, 16)
            load_pairs(0, 0)
            sp.dma_start(bo_row[:, :], bo.partition_broadcast(P)).then_inc(bo_in, 16)
            sp.dma_start(bqk_col[:, :], bqk).then_inc(late_in, 16)
            sp.dma_start(wr_sb[:, :, :], wr.rearrange("(c p) n -> p c n", p=P)).then_inc(late_in, 16)
            sp.dma_start(bv2_row[:, :], bv2.partition_broadcast(P)).then_inc(late_in, 16)
            sp.dma_start(br_row[:, :], br.partition_broadcast(P)).then_inc(late_in, 16)
            for b in range(2, BLK):
                load_ctx(0, b)
                if b == 3:
                    sp.dma_start(wo_sb[:, :, :], wo.rearrange("(c p) n -> p c n", p=P)).then_inc(wo_in, 16)
                    sp.dma_start(wqkv[:, :, :], wqkv_t.rearrange("(c p) n -> p c n", p=P)).then_inc(wqkv_in, 16)
                if b == 5:
                    sp.wait_ge(zeroed, 1)
                    zeros = s2[:, :, :].rearrange("p h k -> p (h k)")[:, 0:D]
                    for i in range(STEPS):
                        sp.dma_start(slots_x[i * P:(i + 1) * P, :], zeros).then_inc(xs_zeroed, 16)
                load_pairs(0, b - 1)
            with sp.Fori(1, NB) as n:
                load_ctx(n, 0)
                load_pairs(n, -1)
                load_ctx(n, 1)
                for b in range(BLK - 1):
                    load_pairs(n, b, range(1))
                    if b == BLK - 2:
                        local_heads(n - 1)
                    load_pairs(n, b, range(1, TPB))
                    if b + 2 < BLK:
                        load_ctx(n, b + 2)
            load_pairs(NB - 1, BLK - 1)

            def load_up(s, e, arrived):
                sp.dma_start(w1_sb[s][:, :, :], w1[e].rearrange("(c p) h -> p c h", p=P)).then_inc(arrived, 16)
                sp.dma_start(b1_sb[s][:, :], b1[e]).then_inc(arrived, 16)

            def load_down(s, e, arrived):
                sp.dma_start(w2_sb[s][:, :, :], w2[e].rearrange("(j p) d -> p j d", p=P)).then_inc(arrived, 16)
                sp.dma_start(b2_sb[s][:, :], b2[e].partition_broadcast(P)).then_inc(arrived, 16)

            def load_slots(s, i, arrived):
                sp.dma_start(xs[s][:, :], slots_x[i * P:(i + 1) * P, :] if isinstance(i, int)
                             else slots_x.rearrange("(i p) d -> i p d", p=P)[i]).then_inc(arrived, 16)

            sp.wait_ge(v_done, NB * T)
            sp.wait_ge(s_done, NB * T * G)
            sp.wait_ge(pv_done, NB * T)
            for s in range(2):
                load_up(s, s, up_in[s])
                load_down(s, s, down_in[s])
            local_heads(NB - 1)
            sp.wait_ge(scattered, NB * 16)
            load_slots(0, 0, xs_in[0])
            load_slots(1, 1, xs_in[1])
            sp.wait_ge(plan_ready, 1)
            n_over = sp.value_load(plan_i[0:1, OVER:OVER + 1], min_val=0, max_val=OVER)
            with sp.If(n_over > 0):
                e = sp.value_load(plan_i[0:1, 0:1], min_val=0, max_val=E - 1)
                load_up(2, e, o_w_in)
                load_down(2, e, o_w_in)
                load_slots(2, E, o_xs_in)
            with sp.Fori(1, E // 2) as i:
                for s in range(2):
                    sp.wait_ge(ht_ready, 4 * i + 2 * s - 2)
                    load_up(s, 2 * i + s, up_in[s])
                    load_slots(s, 2 * i + s, xs_in[s])
                    sp.wait_ge(y_ready, 2 * i + s - 1)
                    load_down(s, 2 * i + s, down_in[s])
            with sp.If(n_over > 1):
                with sp.Fori(1, n_over) as i:
                    sp.wait_ge(y_ready, i + E)
                    e = sp.value_load(plan_i[0:1, bass.ds(i, 1)], min_val=0, max_val=E - 1)
                    load_up(2, e, o_w_in)
                    load_down(2, e, o_w_in)
                    load_slots(2, i + E, o_xs_in)
            for n in range(NB):
                sp.wait_ge(out_ready, n + 1)
                sp.dma_start(out[n], yg[:, n, :]).then_inc(stored, 16)
            sp.wait_ge(stored, NB * 16)

        @block.gpsimd
        def _(pool):
            nc.gpsimd.memset(ident[:, :], 0.0).then_inc(pool_own, 1)
            nc.gpsimd.memset(ones[:, :], 1.0).then_inc(pool_own, 1)
            nc.gpsimd.memset(power[:, :], -0.5).then_inc(pool_own, 1)
            pool.wait_ge(pool_own, 3)
            nc.gpsimd.affine_select(out=ident[:, :], in_=ident[:, :], compare_op=ALU.not_equal, fill=1.0,
                                    base=0, pattern=[[-1, P]], channel_multiplier=1).then_inc(masks, 1)
            nc.gpsimd.affine_select(out=before[:, :], in_=ones[:, :], compare_op=ALU.is_gt, fill=0.0,
                                    base=0, pattern=[[1, P]], channel_multiplier=-1).then_inc(masks, 1)

            def inverse_root(k):
                pool.wait_ge(var_ready, k + 1)
                nc.gpsimd.tensor_tensor(out=rstd[:, :], in0=var_eps[:, :], in1=power[:, :], op=ALU.pow
                                        ).then_inc(rstd_ready, 1)

            nc.gpsimd.memset(qd_hi[:, :, :].bitcast(F32), 0.0).then_inc(qd_zeroed, 1)
            nc.gpsimd.memset(qd_both[:, :, :].bitcast(F32), 0.0).then_inc(qd_zeroed, 1)
            inverse_root(0)

            def split_low(n, b):
                wait(pool, ctx_high, n * BLK + b + 1)
                nc.gpsimd.tensor_tensor(out=ctx_lo[:, b % 2, :], in0=ctx_raw[:, b % 2, :],
                                        in1=ctx_hi[:, b % 2, :].bitcast(F32), op=ALU.subtract
                                        ).then_inc(ctx_split, 1)

            def scale_v(n, t):
                pool.wait_ge(v_ready, n * T + t + 1)
                pool.wait_ge(rz_ready, n * T + t + 1)
                wait(pool, pv_done, n * T + t - 1)
                nc.gpsimd.tensor_tensor(
                    out=v_scaled[:, t % 2, :].rearrange("p (h d) -> p h d", d=DH),
                    in0=v_raw[:, t % 4, :].rearrange("p (h d) -> p h d", d=DH),
                    in1=rz[:, t % 2, :].unsqueeze(2).to_broadcast([P, H, DH]), op=ALU.mult).then_inc(vs_ready, 1)

            def batch(n, first):
                if first < 0:
                    split_low(n, 0)
                for t in range(first, AFTER):
                    scale_v(n, t)
                    if t % 2 == 0 and t // 2 + 2 < BLK:
                        split_low(n, t // 2 + 2)
                    if first < 0 and t in (AT_WO // 2 - 1, AT_X2_IN // 2 - 1):
                        inverse_root(2 * n + NB - 2 + (t > 0))
                    if first == 0 and 2 * t + 2 in AT_NORM:
                        inverse_root(AT_NORM[2 * t + 2])
                    if first == 0 and t == AT_BIAS // 2 - 1:
                        pool.wait_ge(bo_in, 16)
                        pool.wait_ge(xn_ready, NB)
                        nc.gpsimd.tensor_tensor(out=x_sb[:, :, :], in0=x_sb[:, :, :],
                                                in1=bo_row[:, :].unsqueeze(1).to_broadcast([P, NB, D]), op=ALU.add
                                                ).then_inc(x_biased, 1)
                        pool.wait_ge(q_done, NB)
                        nc.gpsimd.memset(p_pad[:, :, :], 0.0).then_inc(p_zeroed, 1)

            split_low(0, 0)
            nc.gpsimd.memset(s2[:, :, :], 0.0).then_inc(zeroed, 1)
            nc.gpsimd.memset(kd[:, :, :], 0.0).then_inc(kd_zeroed, 1)
            split_low(0, 1)
            pool.wait_ge(zeroed, 1)
            ys = slots_y.rearrange("(i p) d -> i p d", p=P)
            zeros = s2[:, :, :].rearrange("p h k -> p (h k)")[:, 0:D]
            for arrived, i in ((y_out[0], E), (y_out[1], E + 1), (y_zeroed, E + 2)):
                pool.dma_start(ys[i], zeros).then_inc(arrived, 16)
            batch(0, 0)
            with pool.Fori(1, NB) as n:
                batch(n, FIRST)
            for t in range(AFTER, T):
                scale_v(NB - 1, t)
            inverse_root(3 * NB - 2)
            inverse_root(3 * NB - 1)

            pool.wait_ge(xs_zeroed, 16 * STEPS)
            pool.wait_ge(y_zeroed, 16)
            pool.wait_ge(xf_ready, 1)
            for n in range(NB):
                nc.gpsimd.indirect_dma_start(
                    out=slots_x, out_offset=bass.IndirectOffsetOnAxis(ap=slot_i[:, n:n + 1].bitcast(U32), axis=0),
                    in_=xf[:, n, :], in_offset=None).then_inc(scattered, 16)
            with pool.Fori(0, E // 2) as i:
                for s in range(2):
                    pool.wait_ge(y_ready, 2 * i + s + 1)
                    pool.dma_start(ys[2 * i + s], y_sb[s][:, :]).then_inc(y_out[s], 16)
            for s in range(2):
                pool.wait_ge(y_out[s], 16 * (E // 2 + 1))
            n_over = pool.value_load(plan_i[0:1, OVER:OVER + 1], min_val=0, max_val=OVER)
            with pool.If(n_over > 0):
                with pool.Fori(0, n_over) as i:
                    pool.wait_ge(y_ready, i + E + 1)
                    pool.dma_start(ys[i + E], y_sb[0][:, :]).then_inc(y_out[0], 16)
                    pool.wait_ge(y_out[0], i * 16 + 16 + 16 * (E // 2 + 1))
            for n in range(NB):
                nc.gpsimd.indirect_dma_start(
                    out=yg[:, n, :], out_offset=None, in_=slots_y,
                    in_offset=bass.IndirectOffsetOnAxis(ap=slot_i[:, n:n + 1].bitcast(U32), axis=0)
                ).then_inc(gathered[n], 16)

        @block.scalar
        def _(act):
            def exps(n, t):
                wait(act, pv_done, n * T + t - 1)
                for g in range(G):
                    act.wait_ge(max_done, n * T * G + t * G + g + 1)
                    for k in range(G):
                        h = G * g + k
                        last = nc.scalar.activation(e_sb[:, t % 2, h * L:(h + 1) * L], ps_s[g][:, k, :], ACT.Exp,
                                                    bias=nmax[:, t % 2, h:h + 1], scale=1.0,
                                                    accum_out=zsum[:, t % 2, h:h + 1])
                    last.then_inc(exp_done, 1)

            def split_high(n, b):
                act.wait_ge(ctx_in[b % 2], (n * (BLK // 2) + b // 2) * 16 + 16)
                wait(act, v_done, n * T + TPB * (b - 1))
                nc.scalar.activation(ctx_hi[:, b % 2, :], ctx_raw[:, b % 2, :], ACT.Copy).then_inc(ctx_high, 1)

            def local_exp(n):
                act.wait_ge(p_zeroed, 1)
                for i in range(2):
                    some = slice(i * H // 2, (i + 1) * H // 2)
                    act.wait_ge(s2_ready, 2 * n + i + 1)
                    for a in range(2):
                        r = slice(HALF * a, HALF * (a + 1))
                        last = nc.scalar.activation(p_pad[r, some, HALF * a:HALF * (a + 1)], s2[r, some, :], ACT.Exp,
                                                    scale=SCALE)
                    last.then_inc(p2_exp, 1)

            def take_x2(n):
                act.wait_ge(tr_done, 2 * n + 2)
                nc.scalar.activation(xn_t[:, :, :], ps_m4, ACT.Copy).then_inc(tr_ready, 1)

            def batch(n, first):
                if first < 0:
                    split_high(n, 0)
                for t in range(first, AFTER):
                    exps(n, t)
                    if t % 2 == 0 and t // 2 + 2 < BLK:
                        split_high(n, t // 2 + 2)
                    if first < 0 and t == AT_SUM // 2 - 1:
                        local_exp(n - 1)
                if first < 0:
                    take_x2(n - 1)

            split_high(0, 0)
            split_high(0, 1)
            batch(0, 0)
            with act.Fori(1, NB) as n:
                batch(n, FIRST)
            for t in range(AFTER, T):
                exps(NB - 1, t)
            local_exp(NB - 1)
            take_x2(NB - 1)

            act.wait_ge(lg_ready, 1)
            nc.scalar.activation(r_b[:, :, :], r_a[:, :, :], ACT.Exp).then_inc(lg_ready, 1)

        @block.vector
        def _(dve):
            own = [0, 0]

            def link(ins):
                own[1] += 1
                ins.then_inc(dve_own, 1)
                dve.wait_ge(dve_own, own[0] + own[1])

            def norm(row, k, ready):
                link(nc.vector.tensor_reduce(mv[:, 0:1], row, AX, ALU.add))
                link(nc.vector.tensor_scalar(mv[:, 0:1], mv[:, 0:1], 1.0 / D, None, ALU.mult))
                link(nc.vector.tensor_scalar(xn[:, :], row, mv[:, 0:1], None, ALU.subtract))
                link(nc.vector.tensor_tensor_reduce(out=mixed[:, :], in0=xn[:, :], in1=xn[:, :], scale=1.0, scalar=0.0,
                                                    op0=ALU.mult, op1=ALU.add, accum_out=mv[:, 1:2]))
                nc.vector.tensor_scalar(var_eps[:, :], mv[:, 1:2], 1.0 / D, EPS, ALU.mult, ALU.add
                                        ).then_inc(var_ready, 1)
                dve.wait_ge(rstd_ready, k + 1)
                nc.vector.tensor_scalar(xn[:, :], xn[:, :], rstd[:, :], None, ALU.mult).then_inc(ready, 1)

            def take_xt(n):
                dve.wait_ge(xt_done, n + 1)
                wait(dve, q_done, n)
                nc.vector.tensor_copy(xn_t[:, :, :], ps_m4).then_inc(xt_ready, 1)

            def take_q(n):
                dve.wait_ge(q_done, n + 1)
                for g in range(G):
                    last = nc.vector.tensor_scalar(qf[:, g, n * L:(n + 1) * L], ps_m4[:, g, :], bq_col[:, g:g + 1],
                                                   SCALE, ALU.add, ALU.mult)
                last.then_inc(qf_ready, 1)

            def prepare(place):
                if place in AT_NORM:
                    n = AT_NORM[place]
                    dve.wait_ge(x_in, 16)
                    norm(x_sb[:, n, :], n, xn_ready)
                if place - 2 in AT_NORM:
                    take_xt(AT_NORM[place - 2])
                if place - 3 in AT_NORM:
                    take_q(AT_NORM[place - 3])

            def split_weights(i, arrived, hi, lo, parts):
                dve.wait_ge(arrived, 16)
                for part in range(parts):
                    cols = slice(part * D // parts, (part + 1) * D // parts)
                    link(nc.vector.tensor_copy(hi[:, :, cols], wkv_raw[:, i, :, cols]))
                    nc.vector.tensor_tensor(lo[:, :, cols], wkv_raw[:, i, :, cols], hi[:, :, cols].bitcast(F32),
                                            ALU.subtract).then_inc(wkv_split, 1)

            def queries(n):
                wait(dve, s_done, n * T * G)
                dve.wait_ge(qd_zeroed, 2)
                dve.wait_ge(qf_ready, n + 1) if isinstance(n, int) else dve.wait_ge(qf_ready, NB)
                for k in range(G):
                    r = slice(DH * k, DH * (k + 1))
                    for qd in (qd_hi, qd_both):
                        last = nc.vector.tensor_scalar(qd[r, :, k * L:(k + 1) * L], qf[r, :, bass.ds(n * L, L)], 1.0,
                                                       None, ALU.mult)
                link(last)
                for k in range(G):
                    r = slice(DH * k, DH * (k + 1))
                    away = (DH * k + HALF) % P
                    last = nc.vector.tensor_tensor(qd_both[away:away + DH, :, k * L:(k + 1) * L],
                                                   qf[r, :, bass.ds(n * L, L)],
                                                   qd_hi[r, :, k * L:(k + 1) * L].bitcast(F32), ALU.subtract)
                last.then_inc(qd_ready, 1)

            def take_k(n, b):
                wait(dve, s_done, n * T * G + TPB * G * (b - 1))
                for i in range(2):
                    dve.wait_ge(k_done, n * 2 * BLK + 2 * b + i + 1)
                    for m in range(2):
                        c = 2 * i + m
                        last = nc.vector.tensor_scalar(kt_hi[:, b % 2, c, :], ps_proj[i][:, m * SB:(m + 1) * SB],
                                                       bk_col[:, c:c + 1], None, ALU.add)
                    link(last)
                    for m in range(2):
                        c = 2 * i + m
                        last = nc.vector.scalar_tensor_tensor(
                            kt_lo[:, b % 2, c, :], ps_proj[i][:, m * SB:(m + 1) * SB], bk_col[:, c:c + 1],
                            kt_hi[:, b % 2, c, :].bitcast(F32), ALU.add, ALU.subtract)
                    last.then_inc(k_ready, 1)

            def take_v(n, t):
                dve.wait_ge(v_done, n * T + t + 1)
                wait(dve, vs_ready, n * T + t - 3)
                nc.vector.tensor_tensor(v_raw[:, t % 4, :], ps_proj[t % 2][:, :], bv_row[:, :], ALU.add
                                        ).then_inc(v_ready, 1)

            def maxima(n, t):
                for g in range(G):
                    dve.wait_ge(s_done, n * T * G + t * G + g + 1)
                    nc.vector.tensor_reduce(nmax[:, t % 2, G * g:G * (g + 1)], ps_s[g][:, :, :], AX, ALU.max,
                                            negate=True).then_inc(max_done, 1)

            def sums(n, t):
                dve.wait_ge(exp_done, n * T * G + (t + 1) * G)
                nc.vector.reciprocal(rz[:, t % 2, :], zsum[:, t % 2, :]).then_inc(rz_ready, 1)

            def take_attn(n):
                dve.wait_ge(xs_zeroed, 16 * STEPS)
                dve.wait_ge(y_zeroed, 16)
                dve.wait_ge(y_out[0], 16)
                dve.wait_ge(y_out[1], 16)
                dve.wait_ge(pv_done, n * T + T)
                nc.vector.tensor_copy(attn_t[:, :, :], ps_pv[:, :, :]).then_inc(attn_ready, 1)

            def local(n, place):
                row = cur[:, :]
                last_batch = isinstance(n, int)

                def in_bank(g):
                    return ps_s[g][:, :, :] if last_batch else ps_m4

                if place == AT_WO:
                    dve.wait_ge(wo_done, n + 1)
                    dve.wait_ge(x_biased, 1)
                    dve.wait_ge(late_in, 4 * 16)
                    link(nc.vector.tensor_tensor(row, x_sb[:, n, :], ps_m[:, :], ALU.add))
                    norm(row, 2 * n + NB, x1n_ready)
                if place == AT_X1:
                    dve.wait_ge(tr_done, 2 * n + 1)
                    nc.vector.tensor_copy(xn_t[:, :, :], ps_m4).then_inc(tr_ready, 1)
                if place == AT_Q:
                    dve.wait_ge(qkv2_done, 3 * n + 1)
                    nc.vector.tensor_tensor(q2t[:, :, :], ps_m4, bqk_col[:, 0:C].unsqueeze(2).to_broadcast([P, C, L]),
                                            ALU.add).then_inc(qkv2_ready, 1)
                if place == AT_K:
                    dve.wait_ge(qkv2_done, 3 * n + 2)
                    dve.wait_ge(kd_zeroed, 1)
                    for k in range(G):
                        r = slice(DH * k, DH * (k + 1))
                        last = nc.vector.tensor_tensor(kd[r, :, k * L:(k + 1) * L], ps_m4[r],
                                                       bqk_col[r, C:2 * C].unsqueeze(2).to_broadcast([DH, C, L]),
                                                       ALU.add)
                    last.then_inc(qkv2_ready, 1)
                if place == AT_V:
                    dve.wait_ge(qkv2_done, 3 * n + 3)
                    nc.vector.tensor_tensor(v2[:, :], ps_m[:, :], bv2_row[:, :], ALU.add).then_inc(qkv2_ready, 1)
                if AT_S <= place < AT_S + G:
                    g = place - AT_S
                    dve.wait_ge(s2_done, n * G + g + 1)
                    nc.vector.tensor_copy(s2[0:HALF, G * g:G * (g + 1), :], in_bank(g)[0:HALF, :, 0:HALF])
                    nc.vector.tensor_copy(s2[HALF:P, G * g:G * (g + 1), :], in_bank(g)[HALF:P, :, HALF:L]
                                          ).then_inc(s2_read, 1)
                if place in (AT_S + 1, AT_S + G - 1):
                    done = place - AT_S + 1
                    some = slice(G * (done - 2), G * done)
                    dve.wait_ge(s2_read, n * G + done)
                    link(nc.vector.tensor_reduce(nm2[:, some], s2[:, some, :], AX, ALU.max, negate=True))
                    nc.vector.tensor_tensor(s2[:, some, :], s2[:, some, :],
                                            nm2[:, some].unsqueeze(2).to_broadcast([P, H // 2, HALF]),
                                            ALU.add).then_inc(s2_ready, 1)

                def sum_up():
                    dve.wait_ge(p2_exp, 2 * n + 2)
                    for a in range(2):
                        r = slice(HALF * a, HALF * (a + 1))
                        last = nc.vector.tensor_reduce(z2[r, :], p_pad[r, :, HALF * a:HALF * (a + 1)], AX, ALU.add)
                    link(last)
                    link(nc.vector.reciprocal(rz2[:, :], z2[:, :]))

                if place == AT_SUM and not last_batch:
                    sum_up()

                def take_p(g):
                    dve.wait_ge(pt_done, n * G + g + 1)
                    nc.vector.tensor_copy(p_t_last[:, g] if last_batch else p_t[:, :, :], in_bank(g)
                                          ).then_inc(pt_ready, 1)

                def take_heads(g):
                    dve.wait_ge(o2_done, n * G + g + 1)
                    nc.vector.tensor_copy(attn_t[:, g, :], in_bank(g)[:, 0, :]).then_inc(ot_ready, 1)

                if not last_batch and AT_P <= place < AT_P + 2 * G:
                    g = (place - AT_P) // 2
                    take_heads(g) if (place - AT_P) % 2 else take_p(g)
                if last_batch and place == AT_P:
                    for g in range(G):
                        if g == G // 2:
                            sum_up()
                        take_p(g)
                    for g in range(G):
                        take_heads(g)
                if place == AT_O:
                    dve.wait_ge(ot_done, n + 1)
                    wait(dve, heads_out, n * 16)
                    nc.vector.tensor_tensor(o2[:, :].rearrange("p (h d) -> p h d", d=DH),
                                            ps_m[:, :].rearrange("p (h d) -> p h d", d=DH),
                                            rz2[:, :].unsqueeze(2).to_broadcast([P, H, DH]), ALU.mult
                                            ).then_inc(o2_read, 1)
                if place == AT_X2_IN:
                    dve.wait_ge(heads_in, n * 16 + 16)
                    link(nc.vector.tensor_tensor(row, row, mixed[:, :], ALU.add))
                    norm(row, 2 * n + NB + 1, x1n_ready)
                    nc.vector.tensor_scalar(x_sb[:, n, :], row, 1.0, None, ALU.mult)
                    nc.vector.tensor_scalar(mean_all[:, bass.ds(n, 1)], mv[:, 0:1], 1.0, None, ALU.mult)
                    link(nc.vector.tensor_scalar(rstd_all[:, bass.ds(n, 1)], rstd[:, :], 1.0, None, ALU.mult))
                if place == AT_LG:
                    dve.wait_ge(lg_done, n + 1)
                    nc.vector.tensor_tensor(logits[:, n, :], ps_m[:, 0:E], br_row[:, :], ALU.add).then_inc(lg_taken, 1)

            def batch(n, first):
                for t in range(first, AFTER):
                    b = t // 2 + 1
                    maxima(n, t)
                    if t or first:
                        sums(n, t - 1)
                    if t == -1:
                        queries(n)
                    if first == 0:
                        prepare(2 * t)
                    if first < 0:
                        local(n - 1, 2 * t)
                    if t % 2 == 0:
                        take_k(n, b)
                    else:
                        take_v(n, 2 * b)
                        take_v(n, 2 * b + 1)
                    if first < 0 and t == 0:
                        take_attn(n - 1)
                    if first < 0:
                        local(n - 1, 2 * t + 1)
                    else:
                        prepare(2 * t + 1)

            def chain(value, used):
                own[0], own[1] = value, used

            dve.wait_ge(x0_in, 16)
            norm(x_sb[:, 0, :], 0, xn_ready)
            split_weights(0, wk_in, wk_hi, wk_lo, 2)
            take_xt(0)
            split_weights(1, wv_in, wv_hi, wv_lo, 1)
            dve.wait_ge(consts_in, 3 * 16)
            take_k(0, 0)
            take_q(0)
            queries(0)
            take_v(0, 0)
            take_v(0, 1)
            batch(0, 0)
            start = own[1]
            with dve.Fori(1, NB) as n:
                chain((n - 1) * DVE_CHAIN + start, 0)
                batch(n, FIRST)
                assert own[1] == DVE_CHAIN, own
            chain(start + (NB - 1) * DVE_CHAIN, 0)
            for t in range(AFTER, T):
                maxima(NB - 1, t)
                sums(NB - 1, t - 1)
                if t == AFTER:
                    take_v(NB - 1, T - 2)
                    take_v(NB - 1, T - 1)
            sums(NB - 1, T - 1)
            take_attn(NB - 1)
            counts = ps_proj[0][:, 0:(NB + 1) * E].rearrange("p (n e) -> p n e", e=E)
            some = NB - 1
            idle = slice(0, some)

            def wide(v, k):
                return v.unsqueeze(2).to_broadcast([P, k, E])

            def normed(n):
                return nc.vector.tensor_scalar(xf[:, n, :], x_sb[:, n, :], mean_all[:, n:n + 1], rstd_all[:, n:n + 1],
                                               ALU.subtract, ALU.mult)

            def route_first():
                nc.vector.memset(oh[:, some:, :], 0.0)
                nc.vector.memset(over_cum[:, :, :], 0.0)
                for e in range(E):
                    last = nc.vector.memset(iota_e[:, e:e + 1], float(e - E))
                link(last)
                dve.wait_ge(lg_taken, some)
                link(nc.vector.tensor_reduce(maxl[:, idle], logits[:, idle, :], AX, ALU.max))
                nc.vector.tensor_tensor(r_a[:, idle, :], logits[:, idle, :], wide(maxl[:, idle], some), ALU.subtract)
                link(nc.vector.tensor_tensor(oh[:, idle, :], logits[:, idle, :], wide(maxl[:, idle], some), ALU.is_ge))
                iota_w = iota_e[:, :].unsqueeze(1).to_broadcast([P, some, E])
                link(nc.vector.tensor_tensor(oh_idx[:, idle, :], oh[:, idle, :], iota_w, ALU.mult))
                link(nc.vector.tensor_reduce(chosen[:, idle], oh_idx[:, idle, :], AX, ALU.min))
                nc.vector.tensor_tensor(oh[:, idle, :], iota_w, wide(chosen[:, idle], some), ALU.is_equal
                                        ).then_inc(oh_ready, 1)
                for n in range(some):
                    normed(n)
                dve.wait_ge(pref_done, 1)
                link(nc.vector.tensor_tensor(oh_idx[:, idle, :], oh[:, idle, :], counts[:, idle, :], ALU.mult))
                link(nc.vector.tensor_reduce(rank[:, idle], oh_idx[:, idle, :], AX, ALU.add))

            for place in range(2 * AFTER):
                if place == AT_X2_IN:
                    route_first()
                local(NB - 1, place)

            dve.wait_ge(lg_taken, NB)
            mine = slice(some, NB)
            link(nc.vector.tensor_reduce(maxl[:, mine], logits[:, some, :], AX, ALU.max))
            link(nc.vector.scalar_tensor_tensor(oh_idx[:, some, :], logits[:, some, :], maxl[:, mine], iota_e[:, :],
                                                ALU.is_ge, ALU.mult))
            link(nc.vector.tensor_reduce(chosen[:, mine], oh_idx[:, some, :], AX, ALU.min))
            nc.vector.tensor_scalar(oh[:, some, :], iota_e[:, :], chosen[:, mine], None, ALU.is_equal
                                    ).then_inc(oh_ready, 1)
            nc.vector.tensor_scalar(r_a[:, some, :], logits[:, some, :], maxl[:, mine], None, ALU.subtract
                                    ).then_inc(lg_ready, 1)
            nc.vector.tensor_scalar(first_slot[:, :], chosen[:, :], float(P), float(P * E), ALU.mult, ALU.add)
            link(normed(some))
            dve.wait_ge(pref_done, 2)
            cum0, cum1, pad = over_cum[:, 0, :], over_cum[:, 1, :], E // 2
            link(nc.vector.tensor_scalar(cum0[:, pad:], counts[:, NB, :], float(P), None, ALU.is_gt))
            for i in range(1, OVER):
                link(nc.vector.scalar_tensor_tensor(cum0[:, pad:], counts[:, NB, :], float((i + 1) * P),
                                                    cum0[:, pad:], ALU.is_gt, ALU.add))
            for k, (a, b) in enumerate(((cum0, cum1), (cum1, cum0), (cum0, cum1))):
                reach = 1 << k
                ins = nc.vector.tensor_tensor(b[:, pad:], a[:, pad:], a[:, pad - reach:pad - reach + E], ALU.add)
                if k < 2:
                    link(ins)
            link(nc.vector.tensor_tensor(oh_idx[:, some, :], oh[:, some, :], counts[:, some, :], ALU.mult))
            link(nc.vector.tensor_reduce(rank[:, mine], oh_idx[:, some, :], AX, ALU.add))
            link(nc.vector.scalar_tensor_tensor(over_off[:, :], cum1[:, pad - 1:pad - 1 + E], -1.0, iota_e[:, :],
                                                ALU.add, ALU.subtract))
            nc.vector.tensor_tensor(first_slot[:, :], first_slot[:, :], rank[:, :], ALU.add)
            nc.vector.tensor_scalar(beyond[:, :], rank[:, :], float(P), None, ALU.is_ge)
            link(nc.vector.tensor_tensor(oh_idx[:, :, :], oh[:, 0:NB, :],
                                         over_off[:, :].unsqueeze(1).to_broadcast([P, NB, E]), ALU.mult))
            link(nc.vector.tensor_reduce(moved[:, :], oh_idx[:, :, :], AX, ALU.add))
            link(nc.vector.scalar_tensor_tensor(moved[:, :], moved[:, :], float(P), beyond[:, :], ALU.mult, ALU.mult))
            link(nc.vector.tensor_tensor(moved[:, :], moved[:, :], first_slot[:, :], ALU.add))
            nc.vector.tensor_copy(slot_i[:, :], moved[:, :]).then_inc(xf_ready, 1)
            for i in range(OVER):
                last = nc.vector.tensor_scalar(by_i[:, i, :], cum1[:, pad:], float(i), None, ALU.is_le)
            link(last)
            link(nc.vector.tensor_reduce(plan[:, 0:OVER], by_i[:, :, :], AX, ALU.add))
            nc.vector.tensor_copy(plan[:, OVER:OVER + 1], cum1[:, pad + E - 1:pad + E])
            link(nc.vector.tensor_scalar(plan[:, 0:OVER], plan[:, 0:OVER], float(E - 1), None, ALU.min))
            nc.vector.tensor_copy(plan_i[:, :], plan[:, :]).then_inc(plan_ready, 1)
            dve.wait_ge(lg_ready, 2)
            link(nc.vector.tensor_reduce(esum[:, :], r_b[:, :, :], AX, ALU.add))
            nc.vector.reciprocal(rp[:, :], esum[:, :])

            def take_x(k):
                dve.wait_ge(xst_done, k + 1)
                nc.vector.tensor_copy(xs_t[:, :, :], ps_m4).then_inc(xst_ready, 1)

            def take_hidden(s, k, w, w_count):
                dve.wait_ge(w, w_count)
                for i in range(2):
                    dve.wait_ge(ht_done, 2 * k + i + 1)
                    for j in range(4 * i, 4 * i + 4):
                        last = nc.vector.tensor_scalar(h_t[:, j, :], ps_s[2 * (s % 2) + i][:, j % 4, :],
                                                       b1_sb[s][:, j:j + 1], 0.0, ALU.add, ALU.max)
                    last.then_inc(ht_ready, 1)

            def take_y(s, k, w, w_count, stores):
                dve.wait_ge(y_done, k + 1)
                dve.wait_ge(w, w_count)
                wait(dve, y_out[s % 2], stores)
                nc.vector.tensor_tensor(y_sb[s % 2][:, :], ps_pv[:, :, :].rearrange("p g l -> p (g l)"),
                                        b2_sb[s][:, :], ALU.add).then_inc(y_ready, 1)

            def step(s, k, i):
                take_x(k)
                if not isinstance(k, int) or k:
                    take_y(1 - s, k - 1, down_in[1 - s], (i + s) * 32, (i + s) * 16)
                take_hidden(s, k, up_in[s], i * 32 + 32)

            step(0, 0, 0)
            step(1, 1, 0)
            with dve.Fori(1, E // 2) as i:
                step(0, 2 * i, i)
                step(1, 2 * i + 1, i)
            take_y(1, E - 1, down_in[1], E // 2 * 32, E // 2 * 16)
            n_over = dve.value_load(plan_i[0:1, OVER:OVER + 1], min_val=0, max_val=OVER)
            with dve.If(n_over > 0):
                with dve.Fori(0, n_over) as i:
                    take_x(i + E)
                    take_hidden(2, i + E, o_w_in, i * 64 + 64)
                    take_y(2, i + E, o_w_in, i * 64 + 64, i * 16 + 16 * (E // 2 + 1))
            for n in range(NB):
                dve.wait_ge(gathered[n], 16)
                nc.vector.scalar_tensor_tensor(yg[:, n, :], yg[:, n, :], rp[:, n:n + 1], x_sb[:, n, :],
                                               ALU.mult, ALU.add).then_inc(out_ready, 1)

        @block.tensor
        def _(pe):
            mm = nc.tensor.matmul
            pe.wait_ge(masks, 2)

            def transpose_xn(n):
                pe.wait_ge(xn_ready, n + 1)
                wait(pe, qf_ready, n)
                for c in range(C):
                    last = nc.tensor.transpose(ps_m4[:, c, :], xn[:, c * P:(c + 1) * P], ident[:, :])
                last.then_inc(xt_done, 1)

            def make_q(n):
                pe.wait_ge(xt_ready, n + 1)
                pe.wait_ge(wq_in, 16)
                for g in range(G):
                    for c in range(C):
                        last = mm(ps_m4[:, g, :], wq_sb[:, c, g * P:(g + 1) * P], xn_t[:, c, :], start=c == 0,
                                  stop=c == C - 1, skip_group_check=True)
                last.then_inc(q_done, 1)

            def prepare(place):
                if place - 2 in AT_NORM:
                    transpose_xn(AT_NORM[place - 2])
                if place - 3 in AT_NORM:
                    make_q(AT_NORM[place - 3])

            def project_k(n, b):
                pe.wait_ge(ctx_split, n * BLK + b + 1)
                for i in range(2):
                    pe.wait_ge(wkv_split, i + 1)
                    wait(pe, v_ready, n * T + TPB * (b - 1) + i + 1)
                    for m in range(2):
                        cols = slice((2 * i + m) * P, (2 * i + m + 1) * P)
                        k = 0
                        for c in range(C):
                            rows = slice(c * SB, (c + 1) * SB)
                            for w, z in ((wk_hi, ctx_hi), (wk_hi, ctx_lo), (wk_lo, ctx_hi)):
                                last = mm(ps_proj[i][:, m * SB:(m + 1) * SB], w[:, c, cols], z[:, b % 2, rows],
                                          start=k == 0, stop=k == 3 * C - 1, skip_group_check=True)
                                k += 1
                    last.then_inc(k_done, 1)

            def project_v(n, b):
                pe.wait_ge(wkv_split, 3)
                for i in range(TPB):
                    pe.wait_ge(k_ready, n * 2 * BLK + 2 * b + i + 1)
                    k = 0
                    for c in range(C):
                        rows = slice(c * SB + i * P, c * SB + (i + 1) * P)
                        for z, w in ((ctx_hi, wv_hi), (ctx_hi, wv_lo), (ctx_lo, wv_hi)):
                            last = mm(ps_proj[i][:, :], z[:, b % 2, rows], w[:, c, :], start=k == 0,
                                      stop=k == 3 * C - 1)
                            k += 1
                    last.then_inc(v_done, 1)

            def scores(n, t):
                b, rows = t // TPB, slice((t % TPB) * P, (t % TPB + 1) * P)
                pe.wait_ge(qd_ready, n + (t >= 0))
                pe.wait_ge(k_ready, n * 2 * BLK + 2 * (b + 1))
                pe.wait_ge(pair_in[t % 2], (n * (T // 2) + t // 2 + 1) * 64)
                for g in range(G):
                    wait(pe, exp_done, n * T * G + (t - 1) * G + g + 1)
                    mm(ps_s[g][:, :, :].rearrange("p g l -> p (g l)"), kt_lo[:, b % 2, g, rows], qd_hi[:, g, :],
                       start=True, stop=False, skip_group_check=True)
                    for pair in range(2):
                        cols = slice(pair * 2 * L, (pair + 1) * 2 * L)
                        last = mm(ps_s[g][:, :, :].rearrange("p g l -> p (g l)")[:, cols], k_pair[:, t % 2, g, pair, :],
                                  qd_both[:, g, cols], start=False, stop=True, skip_group_check=True)
                    last.then_inc(s_done, 1)

            def weigh(n, t):
                pe.wait_ge(exp_done, n * T * G + (t + 1) * G)
                pe.wait_ge(vs_ready, n * T + t + 1)
                if t == 0:
                    wait(pe, attn_ready, n)
                for g in range(G):
                    for k in range(G):
                        h = G * g + k
                        last = mm(ps_pv[DH * k:DH * (k + 1), g, :], v_scaled[:, t % 2, h * DH:(h + 1) * DH],
                                  e_sb[:, t % 2, h * L:(h + 1) * L], start=t == 0 and g == 0, stop=t % T == T - 1,
                                  skip_group_check=True)
                last.then_inc(pv_done, 1)

            def local(n, place):
                last_batch = isinstance(n, int)

                def in_bank(g):
                    return ps_s[g][:, :, :] if last_batch else ps_m4

                if place == AT_WO:
                    pe.wait_ge(wo_in, 16)
                    pe.wait_ge(attn_ready, n + 1)
                    wait(pe, lg_taken, n)
                    for g in range(G):
                        last = mm(ps_m[:, :], attn_t[:, g, :], wo_sb[:, g, :], start=g == 0, stop=g == G - 1)
                    last.then_inc(wo_done, 1)
                if place in (AT_X1, AT_X2):
                    k = 2 * n + 1 + (place == AT_X2)
                    pe.wait_ge(x1n_ready, k)
                    for c in range(C):
                        last = nc.tensor.transpose(ps_m4[:, c, :], xn[:, c * P:(c + 1) * P], ident[:, :])
                    last.then_inc(tr_done, 1)
                if place in (AT_Q, AT_K):
                    if place == AT_Q:
                        pe.wait_ge(tr_ready, 2 * n + 1)
                        pe.wait_ge(wqkv_in, 16)
                    else:
                        pe.wait_ge(qkv2_ready, 3 * n + 1)
                    for m in range(C):
                        for c in range(C):
                            col = (place - AT_Q) * D + m * P
                            last = mm(ps_m4[:, m, :], wqkv[:, c, col:col + P], xn_t[:, c, :], start=c == 0,
                                      stop=c == C - 1, skip_group_check=True)
                    last.then_inc(qkv2_done, 1)
                if place == AT_V:
                    pe.wait_ge(qkv2_ready, 3 * n + 2)
                    for c in range(C):
                        last = mm(ps_m[:, :], xn_t[:, c, :], wqkv[:, c, 2 * D:3 * D], start=c == 0, stop=c == C - 1)
                    last.then_inc(qkv2_done, 1)
                if AT_S <= place < AT_S + G:
                    g = place - AT_S
                    if g and not last_batch:
                        pe.wait_ge(s2_read, n * G + g)
                    if g == 0:
                        pe.wait_ge(qkv2_ready, 3 * n + 3)
                    mm(in_bank(g).rearrange("p g l -> p (g l)"), q2t[:, g, :], kd[:, g, :], start=True, stop=True
                       ).then_inc(s2_done, 1)

                def transpose_p(g):
                    if g and not last_batch:
                        pe.wait_ge(ot_ready, n * G + g)
                    if g % 2 == 0:
                        pe.wait_ge(p2_exp, 2 * n + g // 2 + 1)
                    for k in range(G):
                        last = nc.tensor.transpose(in_bank(g)[:, k, :], p_pad[:, G * g + k, :], ident[:, :])
                    last.then_inc(pt_done, 1)

                def weigh_local(g):
                    pe.wait_ge(pt_ready, n * G + g + 1)
                    for k in range(G):
                        h = G * g + k
                        last = mm(in_bank(g)[DH * k:DH * (k + 1), 0, :], v2[:, h * DH:(h + 1) * DH],
                                  p_t_last[:, g, k, :] if last_batch else p_t[:, k, :], start=True, stop=True,
                                  skip_group_check=True)
                    last.then_inc(o2_done, 1)

                if not last_batch and AT_P <= place < AT_P + 2 * G:
                    g = (place - AT_P) // 2
                    weigh_local(g) if (place - AT_P) % 2 else transpose_p(g)
                if last_batch and place == AT_P:
                    for g in range(G):
                        transpose_p(g)
                    for g in range(G):
                        weigh_local(g)
                if place == AT_O:
                    pe.wait_ge(ot_ready, n * G + G)
                    for g in range(G):
                        last = nc.tensor.transpose(ps_m4[:, g, :], attn_t[:, g, :], ident[:, :])
                    last.then_inc(ot_done, 1)
                if place == AT_LG:
                    pe.wait_ge(tr_ready, 2 * n + 2)
                    for c in range(C):
                        last = mm(ps_m[:, 0:E], xn_t[:, c, :], wr_sb[:, c, :], start=c == 0, stop=c == C - 1)
                    last.then_inc(lg_done, 1)

            def batch(n, first):
                for t in range(first, AFTER):
                    b = t // 2 + 1
                    scores(n, t)
                    if first < 0:
                        local(n - 1, 2 * t)
                    else:
                        prepare(2 * t)
                    project_v(n, b) if t % 2 else project_k(n, b)
                    if t or first:
                        weigh(n, t - 1)
                    if first < 0:
                        local(n - 1, 2 * t + 1)
                    else:
                        prepare(2 * t + 1)

            transpose_xn(0)
            project_k(0, 0)
            make_q(0)
            project_v(0, 0)
            batch(0, 0)
            with pe.Fori(1, NB) as n:
                batch(n, FIRST)
            for t in range(AFTER, T):
                scores(NB - 1, t)
                if t == AFTER:
                    project_v(NB - 1, BLK - 1)
                weigh(NB - 1, t - 1)
            weigh(NB - 1, T - 1)
            def count(left, n, first, last, start=False):
                return mm(ps_proj[0][:, first * E:last * E], left[:, :],
                          oh[:, n, :].unsqueeze(1).to_broadcast([P, last - first, E]) if n is not None
                          else oh[:, :, :].rearrange("p n e -> p (n e)"),
                          start=start, stop=True, skip_group_check=True)

            def route_first():
                pe.wait_ge(oh_ready, 1)
                count(before, None, 0, NB + 1, start=True)
                for n in range(NB - 1):
                    last = count(ones, n, n + 1, NB + 1)
                last.then_inc(pref_done, 1)

            for place in range(2 * AFTER):
                if place == AT_X2_IN:
                    route_first()
                local(NB - 1, place)
            pe.wait_ge(oh_ready, 2)
            count(before, NB - 1, NB - 1, NB)
            count(ones, NB - 1, NB, NB + 1).then_inc(pref_done, 1)

            def transpose_x(s, k, arrived, count):
                pe.wait_ge(arrived, count)
                wait(pe, xst_ready, k)
                for c in range(C):
                    last = nc.tensor.transpose(ps_m4[:, c, :], xs[s][:, c * P:(c + 1) * P], ident[:, :])
                last.then_inc(xst_done, 1)

            def up(s, k, arrived, count):
                pe.wait_ge(xst_ready, k + 1)
                pe.wait_ge(arrived, count)
                for half in range(2):
                    for j in range(G):
                        cols = slice((G * half + j) * P, (G * half + j + 1) * P)
                        for c in range(C):
                            last = mm(ps_s[2 * (s % 2) + half][:, j, :], w1_sb[s][:, c, cols], xs_t[:, c, :],
                                      start=c == 0, stop=c == C - 1, skip_group_check=True)
                    last.then_inc(ht_done, 1)

            def down(s, k, arrived, count):
                pe.wait_ge(arrived, count)
                wait(pe, y_ready, k)
                for j in range(J):
                    if j % 4 == 0:
                        pe.wait_ge(ht_ready, 2 * k + j // 4 + 1)
                    last = mm(ps_pv[:, :, :].rearrange("p g l -> p (g l)"), h_t[:, j, :], w2_sb[s][:, j, :],
                              start=j == 0, stop=j == J - 1)
                last.then_inc(y_done, 1)

            def step(s, k, i):
                transpose_x(s, k, xs_in[s], i * 16 + 16)
                if not isinstance(k, int) or k:
                    down(1 - s, k - 1, down_in[1 - s], (i + s) * 32)
                up(s, k, up_in[s], i * 32 + 32)

            step(0, 0, 0)
            step(1, 1, 0)
            with pe.Fori(1, E // 2) as i:
                step(0, 2 * i, i)
                step(1, 2 * i + 1, i)
            down(1, E - 1, down_in[1], E // 2 * 32)
            n_over = pe.value_load(plan_i[0:1, OVER:OVER + 1], min_val=0, max_val=OVER)
            with pe.If(n_over > 0):
                with pe.Fori(0, n_over) as i:
                    transpose_x(2, i + E, o_xs_in, i * 16 + 16)
                    up(2, i + E, o_w_in, i * 64 + 64)
                    down(2, i + E, o_w_in, i * 64 + 64)


def kernel(x, ctx_1024, L0_xattn_Wq, L0_xattn_bq, L0_xattn_Wk, L0_xattn_bk, L0_xattn_Wv, L0_xattn_bv, L0_xattn_Wo,
           L0_xattn_bo, L0_attn_w_qkv, L0_attn_b_qkv, L0_ffn_Wr, L0_ffn_br, L0_ffn_W1, L0_ffn_b1, L0_ffn_W2,
           L0_ffn_b2):
    import numpy as np
    import concourse.bacc as bacc
    from concourse.bass_utils import run_bass_kernel_spmd

    a = np.asarray
    cols = lambda v, k: a(v).reshape(k, P).T
    data = {
        "x": a(x),
        "ctx_t": a(ctx_1024).reshape(NB, BLK, SB, C, P).transpose(0, 1, 4, 3, 2).reshape(NB, BLK, P, C * SB),
        "wq": a(L0_xattn_Wq), "bq": cols(L0_xattn_bq, C), "wk": a(L0_xattn_Wk), "bk": cols(L0_xattn_bk, C),
        "wv": a(L0_xattn_Wv), "bv": a(L0_xattn_bv), "wo": a(L0_xattn_Wo), "bo": a(L0_xattn_bo),
        "wqkv_t": a(L0_attn_w_qkv).T, "bqk": cols(a(L0_attn_b_qkv)[:2 * D], 2 * C), "bv2": a(L0_attn_b_qkv)[2 * D:],
        "wr": a(L0_ffn_Wr), "br": a(L0_ffn_br), "w1": a(L0_ffn_W1),
        "b1": a(L0_ffn_b1).reshape(E, J, P).transpose(0, 2, 1), "w2": a(L0_ffn_W2), "b2": a(L0_ffn_b2),
    }
    nc = bacc.Bacc("TRN2", target_bir_lowering=False, num_devices=1)
    arrays, args = {}, []
    for name, v in data.items():
        v = np.ascontiguousarray(v)
        arrays["in_" + name] = v
        args.append(nc.dram_tensor("in_" + name, v.shape, mybir.dt.from_np(v.dtype), kind="ExternalInput").ap())
    args.append(nc.dram_tensor("out_0", (NB, L, D), F32, kind="ExternalOutput").ap())
    program(nc, *args)
    r = run_bass_kernel_spmd(nc, [arrays], core_ids=[0])
    return r.results[0]["out_0"]
```
